# Optimizing a Trainium2 kernel written in Bass

```python
import numpy as np
import jax
import jax.numpy as jnp

def _softmax(x, axis=-1):
    return jax.nn.softmax(x, axis=axis)
def _gelu(x):
    return jax.nn.gelu(x, approximate=True)
def _silu(x):
    return jax.nn.silu(x)
def _sigmoid(x):
    return jax.nn.sigmoid(x)
def _layernorm(x, axis=-1, eps=1e-5):
    m = jnp.mean(x, axis=axis, keepdims=True)
    v = jnp.var(x, axis=axis, keepdims=True)
    return (x - m) / jnp.sqrt(v + eps)
def _scatter_add(tgt, idx, src, axis=0):
    return tgt.at[idx].add(src)
def _segment_sum(src, seg, n):
    return jax.ops.segment_sum(src, seg, n)

kernel_name = 'mk_metaformer_d1_conv_nhwc128_6bc11f'

def setup_inputs(seed: int = 0):
    np.random.seed(seed)
    _w = jnp.asarray
    def _rec_inputs():
        import jax
        import jax.numpy as jnp
        _gk = jax.random.key(seed)
        x = -0.000125 + 0.9999 * jax.random.normal(jax.random.fold_in(_gk, 1), (16, 128, 128, 128), jnp.float32)
        return x
    x = _rec_inputs()
    def _L0_conv_setup():
        import jax, jax.numpy as jnp
        import numpy as np
        B, H, W, C, K, T = (16, 128, 128, 64, 7, 16)
        C2 = 2 * C

        def _pad_and_fft(kr, ki, h, w, k):
            kern = kr + 1j * ki
            ph = (h - k) // 2
            pw = (w - k) // 2
            padded = jnp.pad(kern, ((0, 0), (ph, h - k - ph), (pw, w - k - pw)))
            return jnp.fft.fft2(padded, axes=(-2, -1))
        key = jax.random.key(seed)
        ks = jax.random.split(key, 12)
        d = {'x_ri': jax.random.normal(ks[0], (B, H, W, C2), jnp.float32), 'Wf': jax.random.normal(ks[1], (C2, C2), jnp.float32) * 0.05, 'bf': jnp.zeros((C2,), jnp.float32), 'Wi': jax.random.normal(ks[2], (C2, C2), jnp.float32) * 0.05, 'bi': jnp.zeros((C2,), jnp.float32), 'Wd': jax.random.normal(ks[3], (C2, C2), jnp.float32) * 0.05, 'bd': jnp.zeros((C2,), jnp.float32), 'A_real': jax.random.normal(ks[4], (C, K, K), jnp.float32) * 0.02, 'A_imag': jax.random.normal(ks[5], (C, K, K), jnp.float32) * 0.02, 'B_real': jax.random.normal(ks[6], (C, K, K), jnp.float32) * 0.02, 'B_imag': jax.random.normal(ks[7], (C, K, K), jnp.float32) * 0.02}
        return d
    _L0_conv_all = _L0_conv_setup()
    _L0_conv_in = {k: v for k, v in _L0_conv_all.items() if k in ('Wf', 'bf', 'Wi', 'bi', 'Wd', 'bd', 'A_real', 'A_imag', 'B_real', 'B_imag', )}
    del _L0_conv_all

    def _L0_ffn_setup():
        import jax, jax.numpy as jnp
        import numpy as np
        BN_EPS = 1e-05
        key = jax.random.key(seed)
        k1, k2, k3 = jax.random.split(key, 3)
        B, T, I, H = (64, 2048, 128, 128)
        x = jax.random.normal(k1, (B, T, I), dtype=jnp.float32)
        W = jax.random.normal(k2, (H, I), dtype=jnp.float32) * (1.0 / np.sqrt(I))
        V = jnp.linalg.qr(jax.random.normal(k3, (H, H), dtype=jnp.float32))[0]
        gamma = jnp.ones((H,), dtype=jnp.float32)
        beta = jnp.zeros((H,), dtype=jnp.float32)
        return {'x': x, 'W': W, 'V': V, 'gamma': gamma, 'beta': beta}
    _L0_ffn_all = _L0_ffn_setup()
    _L0_ffn_in = {k: v for k, v in _L0_ffn_all.items() if k in ('W', 'V', 'gamma', 'beta', )}
    del _L0_ffn_all

    return {
        "x": x,
        "L0_conv_Wf": _L0_conv_in["Wf"],
        "L0_conv_bf": _L0_conv_in["bf"],
        "L0_conv_Wi": _L0_conv_in["Wi"],
        "L0_conv_bi": _L0_conv_in["bi"],
        "L0_conv_Wd": _L0_conv_in["Wd"],
        "L0_conv_bd": _L0_conv_in["bd"],
        "L0_conv_A_real": _L0_conv_in["A_real"],
        "L0_conv_A_imag": _L0_conv_in["A_imag"],
        "L0_conv_B_real": _L0_conv_in["B_real"],
        "L0_conv_B_imag": _L0_conv_in["B_imag"],
        "L0_ffn_W": _L0_ffn_in["W"],
        "L0_ffn_V": _L0_ffn_in["V"],
        "L0_ffn_gamma": _L0_ffn_in["gamma"],
        "L0_ffn_beta": _L0_ffn_in["beta"],
    }

def reference(x, L0_conv_Wf, L0_conv_bf, L0_conv_Wi, L0_conv_bi, L0_conv_Wd, L0_conv_bd, L0_conv_A_real, L0_conv_A_imag, L0_conv_B_real, L0_conv_B_imag, L0_ffn_W, L0_ffn_V, L0_ffn_gamma, L0_ffn_beta):
    import jax
    import jax.numpy as jnp
    def _L0_conv_ref(x_ri, Wf, bf, Wi, bi, Wd, bd, A_real, A_imag, B_real, B_imag):
        import jax, jax.numpy as jnp
        import numpy as np
        B, H, W, C, K, T = (16, 128, 128, 64, 7, 16)
        C2 = 2 * C

        def _pad_and_fft(kr, ki, h, w, k):
            kern = kr + 1j * ki
            ph = (h - k) // 2
            pw = (w - k) // 2
            padded = jnp.pad(kern, ((0, 0), (ph, h - k - ph), (pw, w - k - pw)))
            return jnp.fft.fft2(padded, axes=(-2, -1))
        b, h, w, c2 = x_ri.shape
        c = c2 // 2
        k = A_real.shape[-1]
        forget_gate = jax.nn.sigmoid(x_ri @ Wf + bf + 2.0)
        input_gate = jax.nn.sigmoid(x_ri @ Wi + bi)
        delta = jax.nn.softplus(x_ri @ Wd + bd) * 0.1
        A_f = _pad_and_fft(A_real, A_imag, h, w, k)
        B_f = _pad_and_fft(B_real, B_imag, h, w, k)
        A_ri = jnp.concatenate([A_f.real, A_f.imag], 0).transpose(1, 2, 0)[None]
        B_ri = jnp.concatenate([B_f.real, B_f.imag], 0).transpose(1, 2, 0)[None]
        Ar, Ai = (A_ri[..., :c], A_ri[..., c:])
        mag = jnp.sqrt(Ar ** 2 + Ai ** 2 + 1e-08)
        scale = 0.95 * jax.nn.sigmoid(mag) / (mag + 1e-08)
        Ar = Ar * scale
        Ai = Ai * scale
        Br, Bi_ = (B_ri[..., :c], B_ri[..., c:])
        x_r, x_i = (x_ri[..., :c], x_ri[..., c:])
        Bx_r = Br * x_r - Bi_ * x_i
        Bx_i = Br * x_i + Bi_ * x_r
        inp_r = delta[..., :c] * input_gate[..., :c] * Bx_r
        inp_i = delta[..., c:] * input_gate[..., c:] * Bx_i
        fg_r, fg_i = (forget_gate[..., :c], forget_gate[..., c:])

        def step(h_state, _):
            h_r, h_i = h_state
            Ah_r = Ar * h_r - Ai * h_i
            Ah_i = Ar * h_i + Ai * h_r
            return ((fg_r * Ah_r + inp_r, fg_i * Ah_i + inp_i), None)
        h0 = (jnp.zeros_like(x_r), jnp.zeros_like(x_i))
        (h_r, h_i), _ = jax.lax.scan(step, h0, None, length=T)
        return jnp.concatenate([h_r, h_i], axis=-1)

    def _L0_ffn_ref(x, W, V, gamma, beta):
        import jax, jax.numpy as jnp
        import numpy as np
        BN_EPS = 1e-05
        B, T, H = (x.shape[0], x.shape[1], W.shape[0])
        Wx = jnp.einsum('bti,hi->bth', x, W)
        flat = Wx.reshape(B * T, H)
        mean = jnp.mean(flat, axis=0)
        var = jnp.var(flat, axis=0)
        Wx = ((flat - mean) * jax.lax.rsqrt(var + BN_EPS) * gamma + beta).reshape(B, T, H)
        Vt = V.T

        def step(yt, wx_t):
            yt = jax.nn.sigmoid(wx_t + yt @ Vt)
            return (yt, yt)
        y0 = jnp.zeros((B, H), dtype=Wx.dtype)
        _, ys = jax.lax.scan(step, y0, jnp.swapaxes(Wx, 0, 1))
        return jnp.swapaxes(ys, 0, 1)

    def _gn(v, G=32, eps=1e-5):
        B_, H_, W_, C_ = v.shape
        g = v.reshape(B_, H_, W_, G, C_ // G)
        m = jnp.mean(g, axis=(1, 2, 4), keepdims=True)
        s = jnp.var(g, axis=(1, 2, 4), keepdims=True)
        return ((g - m) / jnp.sqrt(s + eps)).reshape(v.shape)

    def _ln_c(v, eps=1e-6):
        m = jnp.mean(v, axis=-1, keepdims=True)
        s = jnp.var(v, axis=-1, keepdims=True)
        return (v - m) / jnp.sqrt(s + eps)

    def _ln_t(v, eps=1e-5):
        m = jnp.mean(v, axis=-1, keepdims=True)
        s = jnp.var(v, axis=-1, keepdims=True)
        return (v - m) / jnp.sqrt(s + eps)

    def _to_tokens(v):
        B_, H_, W_, C_ = v.shape
        return v.reshape(B_, H_ * W_, C_)
    def _from_tokens(t, like):
        return t.reshape(like.shape)

    x = x + _L0_conv_ref(_ln_c(x), L0_conv_Wf, L0_conv_bf, L0_conv_Wi, L0_conv_bi, L0_conv_Wd, L0_conv_bd, L0_conv_A_real, L0_conv_A_imag, L0_conv_B_real, L0_conv_B_imag)
    t = _to_tokens(x)
    t = t + _L0_ffn_ref(_ln_t(t), L0_ffn_W, L0_ffn_V, L0_ffn_gamma, L0_ffn_beta)
    x = _from_tokens(t, x)
    return x


_drawn_inputs = setup_inputs


def setup_inputs(seed=0):
    import zlib

    import numpy as np

    out = dict(_drawn_inputs(seed))
    spreads = {'L0_conv_bf': (0.0, 0.8),
     'L0_conv_bi': (0.0, 0.8),
     'L0_conv_bd': (0.0, 0.8),
     'L0_ffn_gamma': (1.0, 0.55),
     'L0_ffn_beta': (0.0, 0.41)}
    factors = {'L0_conv_Wf': 8.0,
     'L0_conv_Wi': 8.0,
     'L0_conv_Wd': 8.0,
     'L0_conv_A_real': 8.0,
     'L0_conv_A_imag': 8.0,
     'L0_conv_B_real': 8.0,
     'L0_conv_B_imag': 8.0}
    for name, (base, spread) in spreads.items():
        noise = np.random.default_rng([zlib.crc32(name.encode()), seed]).standard_normal(out[name].shape)
        drawn = base * np.exp(spread * noise) if base else spread * noise
        out[name] = jnp.asarray(drawn.astype(out[name].dtype))
    for name, factor in factors.items():
        out[name] = (out[name] * factor).astype(out[name].dtype)
    return out
```

```python
from contextlib import ExitStack

import concourse.bass as bass
from concourse import mybir

F32 = mybir.dt.float32
BF16 = mybir.dt.bfloat16
I32 = mybir.dt.int32
ALU = mybir.AluOpType
ACT = mybir.ActivationFunctionType
AX = mybir.AxisListType

LN1_EPS = 1e-6
LN2_EPS = 1e-5
BN_EPS = 1e-5
SPECTRAL_EPS = 1e-8
SPECTRAL_RADIUS = 0.95

CHUNKS = 32
WARM_BLOCKS = 2
STEP_BLOCK = 8
START_TOL = 2.0 ** -19

CHAIN = ["softplus", "gain", "b_straight", "b_cross", "bx", "inp", "fsum", "trace1", "fprod", "det1",
         "a_straight", "a_cross", "ah", "fah",
         "trace2", "e1", "trace4", "e2", "n4", "b4",
         "k2", "dk2", "n2", "b4e2", "b2", "k1", "dk1", "n1", "b2e1", "b1",
         "matrix_part", "scalar_part", "state", "x1"]
SQUARES = ["trace1_sq", "trace1_half_sq", "det2", "trace2_sq", "trace2_half_sq", "det4", "trace4_half_sq",
           "scalar_coef"]


def metaformer(nc, x, gate_w, gate_b, taps, dft, row_pick, ident_in, ffn_w, ffn_v, gamma, beta, out):
    NB, ROWS, P, C = x.shape
    H = C // 2
    T = ROWS * P
    HB = NB // 2
    NGRP = NB // 4
    L = T // CHUNKS
    SB = STEP_BLOCK
    BLOCKS = L // SB
    COLS = CHUNKS * NB
    HALF = COLS // 2
    NTOK = NB * T
    TILES = CHUNKS
    assert NB * SB == P and C == P and ROWS % 2 == 0 and BLOCKS % 4 == 0 and BLOCKS >= 8 and TILES % 8 == 0

    def chain_at(r, name, half):
        return r * (2 * len(CHAIN)) + (2 * CHAIN.index(name) + half + 1)

    def square_at(r, name, half):
        return r * (2 * len(SQUARES)) + (2 * SQUARES.index(name) + half + 1)

    x1_dram = nc.dram_tensor("x1_dram", [T, NB, C], F32, kind="Internal").ap()

    with ExitStack() as whole:
        def sem(name):
            return whole.enter_context(nc.semaphore(name))

        def keep(name, shape, dt=F32):
            return whole.enter_context(nc.sbuf_tensor(name, shape, dt))

        ident = keep("ident", [P, P])
        gram = keep("gram", [P, C + 1])
        setup_loaded = sem("setup_loaded")
        gram_copied = sem("gram_copied")
        sync_step = sem("sync_step")

        with ExitStack() as ctx:
            def sb(name, shape, dt=F32):
                return ctx.enter_context(nc.sbuf_tensor(name, shape, dt))

            def pb(name, shape):
                return ctx.enter_context(nc.psum_tensor(name, shape, F32))

            X = [sb(f"x_row{i}", [P, NB, C]) for i in range(2)]
            X1 = sb("x1_row", [P, NB, C])
            XN = sb("xn", [P, NB, C])
            XNT = sb("xn_t", [P, NB, P])
            FG = sb("forget", [P, NB, C])
            IG = sb("in_gate", [P, NB, C])
            SP = sb("soft", [P, NB, C])
            RL = sb("soft_relu", [P, NB, C])
            PA = sb("prod_a", [P, NB, C])
            PBuf = sb("prod_b", [P, NB, C])
            VV = sb("inp_vec", [P, NB, C])
            LNX = sb("ln_x1", [P, NB, C + 2])
            TR1, DT1, HS1, DT2, TR2, TR4, HS2, DT4, HS4, NN, KK, AC = [
                sb(n, [P, NB, H]) for n in ("trace1", "det1", "half1", "det2", "trace2", "trace4", "half2", "det4",
                                            "half4", "n_coef", "k_coef", "a_coef")]
            stats = sb("stats", [P, 2 * NB, 6])
            eps = sb("eps", [P, 2 * NB])
            inv_c = sb("inv_c", [P, 2 * NB])
            minus_half = sb("minus_half", [P, 2 * NB])
            msum, mdif, vsum, rstd, nmr = [sb(n, [P, 2 * NB]) for n in ("msum", "mdif", "vsum", "rstd", "nmr")]
            E = sb("dft_row", [P, P])
            taps_sb = sb("taps", [P, 4 * H])
            raw = sb("coef_raw", [P, 4 * H])
            mag = sb("mag", [P, H])
            mag2 = sb("mag2", [P, H])
            sig = sb("mag_sig", [P, H])
            msq = sb("mag_sq", [P, 2 * H])
            half_c = sb("half_c", [P, H])
            mag_eps = sb("mag_eps", [P, H])
            radius = sb("radius", [P, H])
            minus_one = sb("minus_one", [P, H])
            coef = [sb(f"coef{i}", [P, 7, H]) for i in range(2)]
            wg = sb("gate_w", [P, 3 * C])
            bias_all = sb("bias_all", [P, 3 * C])
            bias_rest = sb("bias_rest", [P, 3 * C])
            bias_part = sb("bias_part", [P, 3 * C], BF16)
            bias_rows = sb("bias_rows", [P, 3 * C], BF16)
            pick = sb("row_pick", [P, 3])
            ones_bf = sb("ones_bf", [P, P], BF16)

            psT = [pb(f"ps_t{i}", [P, 4, P]) for i in range(2)]
            psG = pb("ps_gate", [P, 4, 512])
            psF = pb("ps_fft", [P, 512])
            psM = pb("ps_gram", [P, 512])

            setup = sem("setup")
            x_loaded = sem("x_loaded")
            dft_loaded = sem("dft_loaded")
            x1_stored = sem("x1_stored")
            stats_ready = sem("stats_ready")
            norm_step = sem("norm_step")
            coef_step = sem("coef_step")
            norm_ready = sem("norm_ready")
            xn_ready = sem("xn_ready")
            xn_turned = sem("xn_turned")
            xnt_ready = sem("xnt_ready")
            gate_sums = sem("gate_sums")
            gate_read = sem("gate_read")
            soft_abs = sem("soft_abs")
            soft_exp = sem("soft_exp")
            soft_ready = sem("soft_ready")
            chain = sem("chain")
            squares = sem("squares")
            lnx_ready = sem("lnx_ready")
            gram_added = sem("gram_added")
            coef_sums = sem("coef_sums")
            coef_raw = sem("coef_raw")
            mag_ready = sem("mag_ready")
            mag_sig = sem("mag_sig")
            coef_ready = sem("coef_ready")

            SETUP_STEPS = 9
            SCALAR_COEF_AFTER = 1

            block = ctx.enter_context(nc.Block())

            def rows(eng, row):
                row(-1, 1)
                row(0, 0)
                with eng.Fori(0, (ROWS - 4) // 2) as i:
                    row(2 * i + 1, 1)
                    row(2 * i + 2, 0)
                for r in range(ROWS - 3, ROWS + 1):
                    row(r, r % 2)

            def fixed(r):
                return isinstance(r, int)

            def has_next(r):
                return not fixed(r) or r + 1 < ROWS

            def has_chain(r):
                return not fixed(r) or 0 <= r < ROWS

            def has_last(r):
                return not fixed(r) or r >= 1


            @block.sync
            def _(sp):
                for dst, src in ((ident[:, :], ident_in), (wg[:, :], gate_w), (taps_sb[:, :], taps),
                                 (pick[:, :], row_pick), (bias_all[:, :], gate_b.partition_broadcast(P))):
                    sp.dma_start(dst, src).then_inc(setup_loaded, 16)

                def load(r, par):
                    for b in (0, HB):
                        sp.dma_start(X[par][:, b:b + HB, :],
                                     x_rows[bass.ds(r, 1), :, b:b + HB].rearrange("o w b c -> w (o b) c")).then_inc(x_loaded, 16)
                    sp.dma_start(E[:, :], dft[bass.ds(r, 1)].rearrange("o k w -> k (o w)")).then_inc(dft_loaded, 16)

                x_rows = x.rearrange("b r w c -> r w b c")
                x1_rows = x1_dram.rearrange("(r w) b c -> r w b c", w=P)

                def row(r, par):
                    if fixed(r) and r < 0:
                        load(0, 0)
                        sp.wait_ge(x_loaded, 32)
                        sp.wait_ge(coef_sums, 1)
                        load(1, 1)
                        return
                    if not has_chain(r):
                        return
                    sp.wait_ge(chain, chain_at(r, "x1", 1))
                    sp.sem_inc(sync_step, 1)
                    if not fixed(r) or r + 2 < ROWS:
                        sp.wait_ge(coef_sums, r + 2)
                        sp.sem_inc(sync_step, 1)
                        load(r + 2, par)
                    sp.dma_start(x1_rows[bass.ds(r, 1)].rearrange("o w b c -> w (o b) c"), X1[:, :, :]).then_inc(x1_stored, 16)

                rows(sp, row)
                sp.wait_ge(x1_stored, 16 * ROWS)

            @block.tensor
            def _(pe):
                pe.wait_ge(setup, SETUP_STEPS)
                pe.wait_ge(setup_loaded, 16 * 5)

                nc.tensor.matmul(psM[:, 0:C + 1], LNX[:, 0, 0:C], LNX[:, 0, 0:C + 1], start=True, stop=False)

                def row(r, par):
                    if has_next(r):
                        pe.wait_ge(dft_loaded, 16 * (r + 2))
                        if not fixed(r) or r >= 0:
                            pe.wait_ge(coef_raw, r + 1)
                        nc.tensor.matmul(psF[:, 0:4 * H], E[:, :], taps_sb[:, :], start=True, stop=True).then_inc(coef_sums, 1)
                        for g in range(NGRP):
                            if g == 0:
                                pe.wait_ge(xn_ready, r + 2)
                            if (not fixed(r) or r >= 0) or g >= 2:
                                pe.wait_ge(xnt_ready, NGRP * (r + 1) + g - 1)
                            for b in range(4):
                                last = nc.tensor.transpose(psT[g % 2][:, b, :], XN[:, 4 * g + b, :], ident[:, :])
                            last.then_inc(xn_turned, 1)
                        for g in range(NGRP):
                            pe.wait_ge(xnt_ready, NGRP * (r + 1) + g + 1)
                            if (not fixed(r) or r >= 0) or g >= 1:
                                pe.wait_ge(gate_read, NGRP * (r + 1) + g)
                            for b in range(4):
                                nc.tensor.matmul(psG[:, b, 0:3 * C], ones_bf[0:32, :], bias_rows[0:32, :], start=True, stop=False)
                                last = nc.tensor.matmul(psG[:, b, 0:3 * C], XNT[:, 4 * g + b, :], wg[:, :], start=False, stop=True)
                            last.then_inc(gate_sums, 1)
                    if has_last(r):
                        pe.wait_ge(lnx_ready, r)
                        for b in range(NB):
                            last = nc.tensor.matmul(psM[:, 0:C + 1], LNX[:, b, 0:C], LNX[:, b, 0:C + 1], start=False,
                                                    stop=fixed(r) and r == ROWS and b == NB - 1)
                        last.then_inc(gram_added, 1)

                rows(pe, row)

            @block.gpsimd
            def _(pool):
                NORM_STEPS, COEF_STEPS = 7, 9
                pool.wait_ge(setup, SETUP_STEPS)
                TT, TS = nc.gpsimd.tensor_tensor, nc.gpsimd.tensor_scalar

                def row(r, par):
                    n = [0]

                    def then(ins, count=norm_step, per_row=NORM_STEPS):
                        n[0] += 1
                        ins.then_inc(count, 1)
                        pool.wait_ge(count, per_row * (r + 1) + n[0])

                    pool.wait_ge(stats_ready, r + 2)
                    TT(msum[:, :], stats[:, :, 1], stats[:, :, 4], ALU.add)
                    TT(mdif[:, :], stats[:, :, 1], stats[:, :, 4], ALU.subtract)
                    then(TT(vsum[:, :], stats[:, :, 2], stats[:, :, 5], ALU.add))
                    then(TT(mdif[:, :], mdif[:, :], minus_half[:, :], ALU.mult))
                    TT(vsum[:, :], vsum[:, :], inv_c[:, :], ALU.mult)
                    then(TT(mdif[:, :], mdif[:, :], mdif[:, :], ALU.mult))
                    then(TT(vsum[:, :], vsum[:, :], mdif[:, :], ALU.add))
                    then(TT(vsum[:, :], vsum[:, :], eps[:, :], ALU.add))
                    if not fixed(r) or 0 <= r < ROWS:
                        pool.wait_ge(xn_ready, r + 1)
                    if not fixed(r) or r >= 2:
                        pool.wait_ge(lnx_ready, r - 1)
                    then(TT(rstd[:, :], vsum[:, :], minus_half[:, :], ALU.pow))
                    then(TT(msum[:, :], msum[:, :], minus_half[:, :], ALU.mult))
                    TT(nmr[:, :], msum[:, :], rstd[:, :], ALU.mult).then_inc(norm_ready, 1)
                    if not has_next(r):
                        return
                    q = coef[(par + 1) % 2]
                    n[0] = 0
                    pool.wait_ge(coef_raw, r + 2)
                    then(TT(msq[:, :], raw[:, 0:2 * H], raw[:, 0:2 * H], ALU.mult), coef_step, COEF_STEPS)
                    then(TT(mag2[:, :], msq[:, 0:H], msq[:, H:2 * H], ALU.add), coef_step, COEF_STEPS)
                    then(TT(mag2[:, :], mag2[:, :], mag_eps[:, :], ALU.add), coef_step, COEF_STEPS)
                    TT(mag[:, :], mag2[:, :], half_c[:, :], ALU.pow).then_inc(mag_ready, 1)
                    pool.wait_ge(mag_ready, r + 2)
                    then(TT(mag2[:, :], mag[:, :], mag_eps[:, :], ALU.add), coef_step, COEF_STEPS)
                    then(TT(mag2[:, :], mag2[:, :], minus_one[:, :], ALU.pow), coef_step, COEF_STEPS)
                    pool.wait_ge(mag_sig, r + 2)
                    then(TT(mag2[:, :], mag2[:, :], sig[:, :], ALU.mult), coef_step, COEF_STEPS)
                    then(TT(mag2[:, :], mag2[:, :], radius[:, :], ALU.mult), coef_step, COEF_STEPS)
                    if not fixed(r) or r >= 1:
                        pool.wait_ge(chain, chain_at(r - 1, "a_cross", 1))
                    TT(q[:, 0, :], raw[:, 0:H], mag2[:, :], ALU.mult)
                    TS(q[:, 5, :], raw[:, 3 * H:4 * H], -1.0, 0.0, ALU.mult, ALU.add)
                    TS(q[:, 4, :], raw[:, 2 * H:3 * H], 1.0, 0.0, ALU.mult, ALU.add)
                    TS(q[:, 6, :], raw[:, 3 * H:4 * H], 1.0, 0.0, ALU.mult, ALU.add)
                    then(TT(q[:, 2, :], raw[:, H:2 * H], mag2[:, :], ALU.mult), coef_step, COEF_STEPS)
                    TT(q[:, 1, :], q[:, 2, :], minus_one[:, :], ALU.mult)
                    TT(msq[:, 0:H], q[:, 0, :], q[:, 0, :], ALU.mult)
                    then(TT(msq[:, H:2 * H], q[:, 2, :], q[:, 2, :], ALU.mult), coef_step, COEF_STEPS)
                    TT(q[:, 3, :], msq[:, 0:H], msq[:, H:2 * H], ALU.add).then_inc(coef_ready, 1)

                rows(pool, row)

            @block.scalar
            def _(act):
                act.wait_ge(setup, SETUP_STEPS)

                def halves(buf, h):
                    return buf[:, h * HB:(h + 1) * HB, :]

                def normalise(dst, src, slot, b):
                    return nc.scalar.activation(dst, src, ACT.Identity, bias=nmr[:, slot + b:slot + b + 1],
                                                scale=rstd[:, slot + b:slot + b + 1])

                def row(r, par):
                    def square(name, dst, src, after, bias=0.0):
                        for h in range(2):
                            act.wait_ge(chain, chain_at(r, after, h))
                            nc.scalar.activation(halves(dst, h), halves(src, h), ACT.Square, bias=bias).then_inc(squares, 1)

                    if has_chain(r):
                        square("trace1_sq", TR2, TR1, "trace1")
                        square("trace1_half_sq", HS1, TR1, "trace1", 0.5)
                        square("det2", DT2, DT1, "det1")
                    if has_next(r):
                        act.wait_ge(norm_ready, r + 2)
                        if not fixed(r) or r >= 0:
                            act.wait_ge(chain, chain_at(r, "b_cross", 1))
                        for b in range(NB):
                            last = normalise(XN[:, b, :], X[(par + 1) % 2][:, b, :], NB, b)
                        last.then_inc(xn_ready, 1)
                    if has_chain(r):
                        square("trace2_sq", TR4, TR2, "trace2")
                        square("trace2_half_sq", HS2, TR2, "trace2", 0.5)
                        square("det4", DT4, DT2, "trace2")
                        square("trace4_half_sq", HS4, TR4, "trace4", 0.5)
                    if has_next(r):
                        act.wait_ge(coef_sums, r + 2)
                        if not fixed(r) or r >= 0:
                            act.wait_ge(coef_ready, r + 1)
                        nc.scalar.activation(raw[:, :], psF[:, 0:4 * H], ACT.Identity).then_inc(coef_raw, 1)
                        for g in range(NGRP):
                            act.wait_ge(xn_turned, NGRP * (r + 1) + g + 1)
                            nc.scalar.activation(XNT[:, 4 * g:4 * g + 4, :], psT[g % 2][:, :, :], ACT.Identity).then_inc(xnt_ready, 1)
                        act.wait_ge(mag_ready, r + 2)
                        nc.scalar.activation(sig[:, :], mag[:, :], ACT.Sigmoid).then_inc(mag_sig, 1)
                        for g in range(NGRP):
                            b = slice(4 * g, 4 * g + 4)
                            act.wait_ge(gate_sums, NGRP * (r + 1) + g + 1)
                            nc.scalar.activation(FG[:, b, :], psG[:, :, 0:C], ACT.Sigmoid)
                            nc.scalar.activation(IG[:, b, :], psG[:, :, C:2 * C], ACT.Sigmoid)
                            nc.scalar.activation(RL[:, b, :], psG[:, :, 2 * C:3 * C], ACT.Relu)
                            nc.scalar.activation(SP[:, b, :], psG[:, :, 2 * C:3 * C], ACT.Abs).then_inc(gate_read, 1)
                            if g == SCALAR_COEF_AFTER and has_chain(r):
                                scalar_coef(r)
                    elif has_chain(r):
                        scalar_coef(r)
                    if has_last(r):
                        act.wait_ge(norm_ready, r + 2)
                        if not fixed(r) or r >= 2:
                            act.wait_ge(gram_added, r - 1)
                        for b in range(NB):
                            last = normalise(LNX[:, b, 0:C], X1[:, b, :], 0, b)
                        last.then_inc(lnx_ready, 1)
                    if has_next(r):
                        act.wait_ge(gate_read, NGRP * (r + 2))
                        for h in range(2):
                            nc.scalar.activation(halves(SP, h), halves(SP, h), ACT.Exp, scale=-1.0).then_inc(soft_exp, 1)
                        for h in range(2):
                            act.wait_ge(soft_exp, 2 * (r + 1) + h + 1)
                            nc.scalar.activation(halves(SP, h), halves(SP, h), ACT.Ln, bias=1.0).then_inc(soft_ready, 1)

                def scalar_coef(r):
                    for h in range(2):
                        act.wait_ge(chain, chain_at(r, "n1", h))
                        nc.scalar.activation(halves(AC, h), halves(NN, h), ACT.Identity, scale=-1.0, bias=1.0).then_inc(squares, 1)

                rows(act, row)

            @block.vector
            def _(v):
                done = [0]

                def step(ins):
                    done[0] += 1
                    ins.then_inc(setup, 1)
                    v.wait_ge(setup, done[0])

                V = nc.vector
                V.memset(stats[:, :, :], 0.0)
                V.memset(eps[:, 0:NB], LN2_EPS)
                V.memset(eps[:, NB:2 * NB], LN1_EPS)
                V.memset(minus_half[:, :], -0.5)
                V.memset(half_c[:, :], 0.5)
                V.memset(inv_c[:, :], 1.0 / C)
                V.memset(mag_eps[:, :], SPECTRAL_EPS)
                V.memset(radius[:, :], SPECTRAL_RADIUS)
                V.memset(minus_one[:, :], -1.0)
                V.memset(ones_bf[:, :], 1.0)
                step(V.memset(LNX[:, :, :], 0.0))
                v.wait_ge(setup_loaded, 16 * 5)
                V.tensor_scalar(taps_sb[64:P, H:2 * H], taps_sb[64:P, H:2 * H], -1.0, None, ALU.mult)
                V.tensor_scalar(taps_sb[64:P, 3 * H:4 * H], taps_sb[64:P, 3 * H:4 * H], -1.0, None, ALU.mult)
                V.memset(LNX[:, :, C:C + 1], 1.0)
                step(V.tensor_scalar(bias_all[:, 0:C], bias_all[:, 0:C], 2.0, None, ALU.add))
                step(V.tensor_copy(bias_part[:, :], bias_all[:, :]))
                V.tensor_tensor(bias_rest[:, :], bias_all[:, :], bias_part[:, :], ALU.subtract)
                step(V.tensor_scalar(bias_rows[:, :], bias_part[:, :], pick[:, 0:1], None, ALU.mult))
                step(V.tensor_copy(bias_part[:, :], bias_rest[:, :]))
                step(V.tensor_tensor(bias_rest[:, :], bias_rest[:, :], bias_part[:, :], ALU.subtract))
                step(V.scalar_tensor_tensor(bias_rows[:, :], bias_part[:, :], pick[:, 1:2], bias_rows[:, :], ALU.mult, ALU.add))
                step(V.tensor_copy(bias_part[:, :], bias_rest[:, :]))
                step(V.scalar_tensor_tensor(bias_rows[:, :], bias_part[:, :], pick[:, 2:3], bias_rows[:, :], ALU.mult, ALU.add))

                def full(buf, h):
                    return buf[:, h * HB:(h + 1) * HB, :].rearrange("p b (k c) -> p b k c", k=2)

                def crossed(buf, h):
                    return full(buf, h)[:, :, ::-1, :]

                def pair(buf, h):
                    return buf[:, h * HB:(h + 1) * HB, :]

                def part(buf, h, k):
                    return full(buf, h)[:, :, k, :]

                def both(buf, h):
                    return pair(buf, h).unsqueeze(2).broadcast_to([P, HB, 2, H])

                def row(r, par):
                    q = coef[par]
                    def cf(k):
                        return q[:, k, :].unsqueeze(1).broadcast_to([P, HB, H])

                    def cf2(k, same):
                        a = q[:, k:k + 1, :].broadcast_to([P, 2, H]) if same else q[:, k:k + 2, :]
                        return a.unsqueeze(1).broadcast_to([P, HB, 2, H])

                    def each(name, make, needs=None, square=None):
                        for h in range(2):
                            if needs:
                                v.wait_ge(chain, chain_at(r, needs, h))
                            if square:
                                v.wait_ge(squares, square_at(r, square, h))
                            make(h).then_inc(chain, 1)

                    STT, TT = V.scalar_tensor_tensor, V.tensor_tensor
                    M, A = ALU.mult, ALU.add
                    if has_chain(r):
                        v.wait_ge(soft_ready, 2 * r + 2)
                        each("softplus", lambda h: TT(full(SP, h), full(SP, h), full(RL, h), A))
                        each("gain", lambda h: STT(full(IG, h), full(SP, h), 0.1, full(IG, h), M, M), "softplus")
                        v.wait_ge(coef_ready, r + 1)
                        each("b_straight", lambda h: TT(full(PA, h), full(XN, h), cf2(4, True), M))
                        each("b_cross", lambda h: TT(full(PBuf, h), crossed(XN, h), cf2(5, False), M))
                        each("bx", lambda h: TT(full(PA, h), full(PA, h), full(PBuf, h), A), "b_cross")
                        each("inp", lambda h: TT(full(VV, h), full(PA, h), full(IG, h), M), "bx")
                        each("fsum", lambda h: TT(pair(KK, h), part(FG, h, 0), part(FG, h, 1), A))
                        each("trace1", lambda h: TT(pair(TR1, h), pair(KK, h), cf(0), M), "fsum")
                        each("fprod", lambda h: TT(pair(AC, h), part(FG, h, 0), part(FG, h, 1), M))
                        each("det1", lambda h: TT(pair(DT1, h), pair(AC, h), cf(3), M), "fprod")
                    if fixed(r) and r >= 0 or not fixed(r):
                        v.wait_ge(norm_ready, r + 1)
                    last = None
                    if has_last(r):
                        v.wait_ge(chain, chain_at(r - 1, "x1", 1))
                        for b in range(NB):
                            last = V.bn_stats(stats[:, b, :], X1[:, b, :])
                    if has_next(r):
                        v.wait_ge(x_loaded, 32 * (r + 2))
                        for b in range(NB):
                            last = V.bn_stats(stats[:, NB + b, :], X[(par + 1) % 2][:, b, :])
                    if last is None:
                        last = V.memset(stats[:, 0:1, :], 0.0)
                    last.then_inc(stats_ready, 1)
                    if not has_chain(r):
                        return
                    each("a_straight", lambda h: TT(full(PA, h), full(VV, h), cf2(0, True), M), "inp")
                    each("a_cross", lambda h: TT(full(PBuf, h), crossed(VV, h), cf2(1, False), M))
                    each("ah", lambda h: TT(full(PA, h), full(PA, h), full(PBuf, h), A), "a_cross")
                    each("fah", lambda h: TT(full(PA, h), full(PA, h), full(FG, h), M), "ah")
                    each("trace2", lambda h: STT(pair(TR2, h), pair(DT1, h), -2.0, pair(TR2, h), M, A), None, "det2")
                    each("e1", lambda h: STT(pair(HS1, h), pair(HS1, h), -0.25, pair(DT1, h), A, ALU.subtract))
                    each("trace4", lambda h: STT(pair(TR4, h), pair(DT2, h), -2.0, pair(TR4, h), M, A), None, "trace2_sq")
                    each("e2", lambda h: STT(pair(HS2, h), pair(HS2, h), -0.25, pair(DT2, h), A, ALU.subtract), None, "trace2_half_sq")
                    each("n4", lambda h: STT(pair(NN, h), pair(TR4, h), 1.0, pair(DT4, h), A, M), "trace4", "det4")
                    each("b4", lambda h: STT(pair(HS4, h), pair(HS4, h), 0.75, pair(DT4, h), A, ALU.subtract), None, "trace4_half_sq")
                    each("k2", lambda h: STT(pair(KK, h), pair(TR2, h), 1.0, pair(HS4, h), A, M), "b4")
                    each("dk2", lambda h: TT(pair(KK, h), pair(KK, h), pair(DT2, h), M), "k2")
                    each("n2", lambda h: TT(pair(KK, h), pair(KK, h), pair(NN, h), A), "dk2")
                    each("b4e2", lambda h: TT(pair(HS4, h), pair(HS4, h), pair(HS2, h), M))
                    each("b2", lambda h: STT(pair(HS2, h), pair(HS4, h), 1.0, pair(NN, h), A, ALU.subtract), "b4e2")
                    each("k1", lambda h: STT(pair(NN, h), pair(TR1, h), 1.0, pair(HS2, h), A, M), "b2")
                    each("dk1", lambda h: TT(pair(NN, h), pair(NN, h), pair(DT1, h), M), "k1")
                    each("n1", lambda h: TT(pair(NN, h), pair(NN, h), pair(KK, h), A), "dk1")
                    each("b2e1", lambda h: TT(pair(HS2, h), pair(HS2, h), pair(HS1, h), M))
                    each("b1", lambda h: STT(pair(HS2, h), pair(HS2, h), 1.0, pair(KK, h), A, ALU.subtract), "b2e1")
                    each("matrix_part", lambda h: TT(full(PA, h), full(PA, h), both(HS2, h), M), "b1")
                    each("scalar_part", lambda h: TT(full(VV, h), full(VV, h), both(AC, h), M), None, "scalar_coef")
                    each("state", lambda h: TT(full(PA, h), full(PA, h), full(VV, h), A), "scalar_part")
                    if has_last(r):
                        v.wait_ge(x1_stored, 16 * r)
                        v.wait_ge(lnx_ready, r)
                    each("x1", lambda h: TT(full(X1, h), full(X[par], h), full(PA, h), A), "state")

                rows(v, row)
                v.wait_ge(gram_added, ROWS)
                V.tensor_copy(gram[:, :], psM[:, 0:C + 1]).then_inc(gram_copied, 1)

        with ExitStack() as ctx:
            def sb(name, shape, dt=F32):
                return ctx.enter_context(nc.sbuf_tensor(name, shape, dt))

            def pb(name, shape):
                return ctx.enter_context(nc.psum_tensor(name, shape, F32))

            XT = [sb(f"x1_block{i}", [P, TILES, C]) for i in range(4)]
            OUT = [sb(f"out_half{i}", [P, TILES // 2, C]) for i in range(2)]
            LN = sb("ln_block", [P, TILES, C])
            LNT = [sb(f"ln_t{i}", [P, CHUNKS, SB, NB]) for i in range(2)]
            Y = [sb(f"y_t{i}", [P, CHUNKS, SB, NB]) for i in range(2)]
            START = sb("start", [P, CHUNKS, NB])
            NEXT = sb("next_start", [P, CHUNKS, NB])
            stats = sb("stats2", [P, TILES, 6])
            eps = sb("eps2", [P, TILES])
            inv_c = sb("inv_c2", [P, TILES])
            minus_half = sb("minus_half2", [P, TILES])
            msum, mdif, vsum, rstd, nmr = [sb(n + "2", [P, TILES]) for n in ("msum", "mdif", "vsum", "rstd", "nmr")]
            w_sb, v_sb, w_t, v_t, prod, ws_t = [sb(n, [P, C]) for n in ("w_sb", "v_sb", "w_t", "v_t", "prod", "ws_t")]
            vec = sb("vec", [P, 16])
            ones = sb("ones", [P, 1])
            worst = sb("worst", [P, 2])
            flag = sb("flag", [1, 2], I32)

            psZ = [[pb(f"ps_z{g}{i}", [P, 512]) for i in range(2)] for g in range(2)]
            psI = [pb(f"ps_in{i}", [P, 4, P]) for i in range(2)]
            psO = [pb(f"ps_out{i}", [P, 4, P]) for i in range(2)]
            LOADED = 16 * (CHUNKS // 8)
            GROUPS = TILES // 4

            loaded2 = sem("loaded2")
            fold = sem("fold")
            fold_pe = sem("fold_pe")
            fold_pool = sem("fold_pool")
            x_block = sem("x_block")
            stats2 = sem("stats2")
            norm2_step = sem("norm2_step")
            norm2 = sem("norm2")
            ln_block = sem("ln_block")
            ln_turned = sem("ln_turned")
            lnt_copied = sem("lnt_copied")
            z_ready = [sem(f"z_ready{g}") for g in range(2)]
            y_ready = [sem(f"y_ready{g}") for g in range(2)]
            y_turned = sem("y_turned")
            added = sem("added")
            out_stored = [sem(f"out_stored{h}") for h in range(2)]
            start_set = sem("start_set")
            check_step = sem("check_step")
            worst_max = sem("worst_max")
            worst_turned = sem("worst_turned")
            flag_set = sem("flag_set")
            verdict_seen = sem("verdict_seen")

            blocks_v = x1_dram.rearrange("(j n t) b c -> n (t b) j c", n=BLOCKS, t=SB)
            out_v = out.rearrange("b r w c -> b (r w) c").rearrange("b (j n t) c -> n t b j c", n=BLOCKS, t=SB)
            FOLD_TURNED, FOLD_PROD, FOLD_VAR, FOLD_SCALED, FOLD_STEPS = 3, 4, 8, 12, 13
            SWEEPS = CHUNKS

            block = ctx.enter_context(nc.Block())

            def q_of(k, n):
                return n if k is None else WARM_BLOCKS + k * BLOCKS + n

            def n_blocks(k):
                return WARM_BLOCKS if k is None else BLOCKS

            def run_blocks(eng, k, body):
                if k is None:
                    for n in range(WARM_BLOCKS):
                        body(n, n % 4)
                    return
                for n in range(4):
                    body(n, (n + WARM_BLOCKS) % 4)
                if BLOCKS > 8:
                    with eng.Fori(1, BLOCKS // 4 - 1) as i:
                        for m in range(4):
                            body(4 * i + m, (m + WARM_BLOCKS) % 4)
                for n in range(BLOCKS - 4, BLOCKS):
                    body(n, (n + WARM_BLOCKS) % 4)

            def sweeps(eng, sweep):
                sweep(None)
                eng.wait_ge(flag_set, 1)
                with eng.Fori(0, SWEEPS) as k:
                    again = eng.value_load(flag[0:1, 0:1], min_val=0, max_val=1)
                    with eng.If(again == 1):
                        sweep(k)
                        eng.wait_ge(flag_set, k + 2)
                        eng.sem_inc(verdict_seen, 1)

            def fixed(n):
                return isinstance(n, int)

            def chunks(g):
                return slice(g * CHUNKS // 2, (g + 1) * CHUNKS // 2)

            @block.sync
            def _(sp):
                sp.dma_start(w_sb[:, :], ffn_w).then_inc(loaded2, 16)
                sp.dma_start(v_sb[:, :], ffn_v).then_inc(loaded2, 16)
                sp.dma_start(vec[:, 0:1], gamma).then_inc(loaded2, 16)
                sp.dma_start(vec[:, 1:2], beta).then_inc(loaded2, 16)

                def sweep(k):
                    def load(n, slot):
                        src = n + (BLOCKS - WARM_BLOCKS) if k is None else n
                        if not (k is None and n == 0):
                            sp.wait_ge(x_block, LOADED * q_of(k, n))
                            sp.sem_inc(sync_step, 1)
                        for j in range(0, CHUNKS, 8):
                            sp.dma_start(XT[slot % 4][:, j:j + 8, :],
                                         blocks_v[bass.ds(src, 1), :, j:j + 8].rearrange("o p j c -> p (o j) c")).then_inc(x_block, 16)

                    if k is None:
                        for n in range(WARM_BLOCKS):
                            load(n, n)
                        return
                    for n in range(4):
                        if n == 0:
                            sp.wait_ge(ln_block, q_of(k, 0))
                            sp.sem_inc(sync_step, 1)
                        load(n, n + WARM_BLOCKS)

                    def store(n, slot):
                        for h in range(2):
                            sp.wait_ge(added, GROUPS * (k * BLOCKS + n) + GROUPS // 2 * (h + 1))
                            sp.sem_inc(sync_step, 1)
                            js = slice(h * TILES // 2, (h + 1) * TILES // 2)
                            for t in range(SB):
                                sp.dma_start(out_v[bass.ds(n, 1), t, :, js, :].rearrange("o b j c -> (o b) j c"),
                                             OUT[h][t * NB:(t + 1) * NB, :, :]).then_inc(out_stored[h], 16)
                        if not (fixed(n) and n + 4 >= BLOCKS):
                            load(n + 4, slot)

                    run_blocks(sp, k, store)
                    for h in range(2):
                        sp.wait_ge(out_stored[h], 16 * SB * BLOCKS * (k + 1))
                        sp.sem_inc(sync_step, 1)

                sp.wait_ge(gram_copied, 1)
                sweeps(sp, sweep)

            @block.gpsimd
            def _(pool):
                TT, TS = nc.gpsimd.tensor_tensor, nc.gpsimd.tensor_scalar
                pool.wait_ge(fold, FOLD_VAR)
                TT(vec[:, 6:7], vec[:, 5:6], minus_half[:, 0:1], ALU.pow).then_inc(fold_pool, 1)

                def sweep(k):
                    def norm(n, slot):
                        q = q_of(k, n)
                        m = [0]

                        def then(ins):
                            m[0] += 1
                            ins.then_inc(norm2_step, 1)
                            pool.wait_ge(norm2_step, 7 * q + m[0])

                        pool.wait_ge(stats2, q + 1)
                        TT(msum[:, :], stats[:, :, 1], stats[:, :, 4], ALU.add)
                        TT(mdif[:, :], stats[:, :, 1], stats[:, :, 4], ALU.subtract)
                        then(TT(vsum[:, :], stats[:, :, 2], stats[:, :, 5], ALU.add))
                        then(TT(mdif[:, :], mdif[:, :], minus_half[:, :], ALU.mult))
                        TT(vsum[:, :], vsum[:, :], inv_c[:, :], ALU.mult)
                        then(TT(mdif[:, :], mdif[:, :], mdif[:, :], ALU.mult))
                        then(TT(vsum[:, :], vsum[:, :], mdif[:, :], ALU.add))
                        then(TT(vsum[:, :], vsum[:, :], eps[:, :], ALU.add))
                        if not (k is None and n == 0):
                            pool.wait_ge(ln_block, q)
                        then(TT(rstd[:, :], vsum[:, :], minus_half[:, :], ALU.pow))
                        then(TT(msum[:, :], msum[:, :], minus_half[:, :], ALU.mult))
                        TT(nmr[:, :], msum[:, :], rstd[:, :], ALU.mult).then_inc(norm2, 1)

                    run_blocks(pool, k, norm)

                sweeps(pool, sweep)

            def per_step(total, steps):
                return [total * (t + 1) // steps - total * t // steps if t < steps else 0 for t in range(SB)]

            IN_AT = per_step(GROUPS, 6)
            OUT_AT = per_step(GROUPS, 8)

            def zcount(k, n, t):
                return SB * q_of(k, n) + t

            def prev(k, n):
                return None if fixed(n) and n == 0 else n - 1

            @block.tensor
            def _(pe):
                pe.wait_ge(loaded2, 64)
                pe.wait_ge(gram_copied, 1)
                nc.tensor.transpose(psI[0][:, 0, :], w_sb[:, :], ident[:, :]).then_inc(fold_pe, 1)
                nc.tensor.transpose(psI[1][:, 1, :], v_sb[:, :], ident[:, :]).then_inc(fold_pe, 1)
                pe.wait_ge(fold, FOLD_TURNED)
                nc.tensor.matmul(psO[0][:, 0, 0:C], gram[:, 0:C], w_t[:, :], start=True, stop=True).then_inc(fold_pe, 1)
                nc.tensor.matmul(psO[1][:, 0, 0:1], w_t[:, :], gram[:, C:C + 1], start=True, stop=True).then_inc(fold_pe, 1)
                pe.wait_ge(fold, FOLD_PROD)
                nc.tensor.matmul(psI[1][:, 0, 0:1], prod[:, :], ones[:, :], start=True, stop=True).then_inc(fold_pe, 1)
                pe.wait_ge(fold, FOLD_SCALED)
                nc.tensor.transpose(psI[0][:, 0, :], prod[:, :], ident[:, :]).then_inc(fold_pe, 1)
                pe.wait_ge(fold, FOLD_STEPS)

                def turn_in(k, n, slot, g):
                    at = GROUPS * q_of(k, n) + g
                    if g == 0:
                        pe.wait_ge(ln_block, q_of(k, n) + 1)
                    if not (k is None and n == 0 and g < 2):
                        pe.wait_ge(lnt_copied, at - 1)
                    for j in range(4):
                        last = nc.tensor.transpose(psI[g % 2][:, j, :], LN[:, 4 * g + j, :], ident[:, :])
                    last.then_inc(ln_turned, 1)

                def turn_out(k, n, slot, g):
                    at = GROUPS * (k * BLOCKS + n) + g
                    if not (fixed(n) and n == 0 and g < 2):
                        pe.wait_ge(added, at - 1)
                    for j in range(4):
                        last = nc.tensor.transpose(psO[g % 2][:, j, :], Y[slot % 2][:, 4 * g + j].rearrange("p t b -> p (t b)"), ident[:, :])
                    last.then_inc(y_turned, 1)

                def input_part(n_slot, g, t, stop=False):
                    nc.tensor.matmul(psZ[g][t % 2][:, 0:HALF], ws_t[:, :], LNT[n_slot % 2][:, chunks(g), t, :], start=True, stop=False)

                def sweep(k):
                    if k is None:
                        pe.wait_ge(start_set, 1)
                    slot0 = 0 if k is None else WARM_BLOCKS % 4
                    for g in range(GROUPS):
                        turn_in(k, 0, slot0, g)
                    pe.wait_ge(lnt_copied, GROUPS * (q_of(k, 0) + 1))
                    for g in range(2):
                        input_part(slot0, g, 0)

                    def steps(n, slot):
                        is_last = fixed(n) and n == n_blocks(k) - 1
                        is_first = fixed(n) and n == 0
                        gi = go = 0
                        for t in range(SB):
                            for g in range(2):
                                if t == 0 and is_first:
                                    rhs = START[:, chunks(g), :]
                                    if k is not None:
                                        pe.wait_ge(start_set, k + 2)
                                else:
                                    pe.wait_ge(y_ready[g], zcount(k, n, t))
                                    src = Y[slot % 2] if t else Y[(slot + 1) % 2]
                                    rhs = src[:, chunks(g), (t - 1) % SB, :]
                                nc.tensor.matmul(psZ[g][t % 2][:, 0:HALF], v_t[:, :], rhs, start=False, stop=True).then_inc(z_ready[g], 1)
                                if t + 1 < SB:
                                    input_part(slot, g, t + 1)
                                elif not is_last:
                                    if g == 0:
                                        pe.wait_ge(lnt_copied, GROUPS * (q_of(k, n) + 2))
                                    input_part(slot + 1, g, 0)
                                if g == 0 and not is_last:
                                    for _ in range(IN_AT[t]):
                                        turn_in(k, n + 1, slot + 1, gi)
                                        gi += 1
                                if g == 1 and not is_first and k is not None:
                                    for _ in range(OUT_AT[t]):
                                        turn_out(k, n - 1, slot + 3, go)
                                        go += 1
                        if is_last and k is not None:
                            pe.wait_ge(y_ready[0], zcount(k, n, SB))
                            pe.wait_ge(y_ready[1], zcount(k, n, SB))
                            for g in range(GROUPS):
                                turn_out(k, n, slot, g)

                    run_blocks(pe, k, steps)
                    if k is not None:
                        pe.wait_ge(check_step, 2 * (k + 1))
                        nc.tensor.transpose(psI[0][0:1, 0, :], worst[:, 0:1], ident[:, :]).then_inc(worst_turned, 1)

                sweeps(pe, sweep)

            @block.scalar
            def _(act):
                act.wait_ge(fold, FOLD_STEPS)

                def copy_in(k, n, slot, g):
                    at = GROUPS * q_of(k, n) + g
                    act.wait_ge(ln_turned, at + 1)
                    nc.scalar.activation(LNT[slot % 2][:, 4 * g:4 * g + 4].rearrange("p j t b -> p j (t b)"), psI[g % 2][:, :, :],
                                         ACT.Identity).then_inc(lnt_copied, 1)

                def sweep(k):
                    slot0 = 0 if k is None else WARM_BLOCKS % 4
                    for g in range(GROUPS):
                        copy_in(k, 0, slot0, g)

                    def steps(n, slot):
                        is_last = fixed(n) and n == n_blocks(k) - 1
                        is_first = fixed(n) and n == 0
                        gi = 0
                        if k is not None and not (fixed(n) and n < 2):
                            act.wait_ge(y_turned, GROUPS * (k * BLOCKS + n - 1))
                        elif k is not None and is_first:
                            act.wait_ge(start_set, k + 2)
                        for t in range(SB):
                            for g in range(2):
                                act.wait_ge(z_ready[g], zcount(k, n, t) + 1)
                                nc.scalar.activation(Y[slot % 2][:, chunks(g), t, :], psZ[g][t % 2][:, 0:HALF].rearrange("p (j b) -> p j b", b=NB),
                                                     ACT.Sigmoid, bias=vec[:, 9:10]).then_inc(y_ready[g], 1)
                                if g == 0 and not is_last:
                                    for _ in range(IN_AT[t]):
                                        copy_in(k, n + 1, slot + 1, gi)
                                        gi += 1

                    run_blocks(act, k, steps)

                sweeps(act, sweep)

            @block.vector
            def _(v):
                V = nc.vector
                TT, STT = V.tensor_tensor, V.scalar_tensor_tensor
                done = [0]

                def step(ins):
                    done[0] += 1
                    ins.then_inc(fold, 1)
                    v.wait_ge(fold, done[0])
                    return done[0]

                V.memset(eps[:, :], LN2_EPS)
                V.memset(inv_c[:, :], 1.0 / C)
                V.memset(minus_half[:, :], -0.5)
                V.memset(ones[:, :], 1.0)
                V.memset(START[:, :, :], 0.0).then_inc(start_set, 1)
                step(V.memset(NEXT[:, :, :], 0.0))
                v.wait_ge(loaded2, 64)
                v.wait_ge(fold_pe, 1)
                step(V.tensor_copy(w_t[:, :], psI[0][:, 0, :]))
                v.wait_ge(fold_pe, 2)
                assert step(V.tensor_copy(v_t[:, :], psI[1][:, 1, :])) == FOLD_TURNED
                v.wait_ge(fold_pe, 3)
                assert step(TT(prod[:, :], psO[0][:, 0, 0:C], w_t[:, :], ALU.mult)) == FOLD_PROD
                v.wait_ge(fold_pe, 4)
                step(V.tensor_scalar(vec[:, 3:4], psO[1][:, 0, 0:1], 1.0 / NTOK, None, ALU.mult))
                step(TT(vec[:, 4:5], vec[:, 3:4], vec[:, 3:4], ALU.mult))
                v.wait_ge(fold_pe, 5)
                step(STT(vec[:, 5:6], psI[1][:, 0, 0:1], 1.0 / NTOK, vec[:, 4:5], ALU.mult, ALU.subtract))
                assert step(V.tensor_scalar(vec[:, 5:6], vec[:, 5:6], 0.0, BN_EPS, ALU.max, ALU.add)) == FOLD_VAR
                v.wait_ge(fold_pool, 1)
                step(TT(vec[:, 7:8], vec[:, 6:7], vec[:, 0:1], ALU.mult))
                step(TT(vec[:, 8:9], vec[:, 3:4], vec[:, 7:8], ALU.mult))
                step(TT(vec[:, 9:10], vec[:, 1:2], vec[:, 8:9], ALU.subtract))
                assert step(V.tensor_scalar(prod[:, :], w_sb[:, :], vec[:, 7:8], None, ALU.mult)) == FOLD_SCALED
                v.wait_ge(fold_pe, 6)
                assert step(V.tensor_copy(ws_t[:, :], psI[0][:, 0, :])) == FOLD_STEPS

                def sweep(k):
                    def statistics(n, slot):
                        q = q_of(k, n)
                        v.wait_ge(x_block, LOADED * (q + 1))
                        if not (k is None and n == 0):
                            v.wait_ge(norm2, q)
                        for j in range(TILES):
                            last = V.bn_stats(stats[:, j, :], XT[slot % 4][:, j, :])
                        last.then_inc(stats2, 1)

                    def normalise(n, slot):
                        q = q_of(k, n)
                        v.wait_ge(norm2, q + 1)
                        if not (k is None and n == 0):
                            v.wait_ge(ln_turned, GROUPS * q)
                        for j in range(TILES):
                            last = V.tensor_scalar(LN[:, j, :], XT[slot % 4][:, j, :], rstd[:, j:j + 1], nmr[:, j:j + 1], ALU.mult, ALU.add)
                        last.then_inc(ln_block, 1)

                    def add(n, slot, g):
                        at = GROUPS * (k * BLOCKS + n) + g
                        half = (2 * g) // GROUPS
                        v.wait_ge(y_turned, at + 1)
                        if g == half * (GROUPS // 2) and not (fixed(n) and n == 0):
                            v.wait_ge(out_stored[half], 16 * SB * (k * BLOCKS + n))
                        o = OUT[half][:, (4 * g) % (TILES // 2):(4 * g) % (TILES // 2) + 4, :]
                        TT(o, XT[slot % 4][:, 4 * g:4 * g + 4, :], psO[g % 2][:, :, :], ALU.add).then_inc(added, 1)

                    slot0 = 0 if k is None else WARM_BLOCKS % 4
                    statistics(0, slot0)
                    normalise(0, slot0)
                    statistics(1, slot0 + 1)
                    normalise(1, slot0 + 1)

                    def period(n, slot):
                        if not (fixed(n) and n + 2 >= n_blocks(k)):
                            statistics(n + 2, slot + 2)
                        if k is not None and not (fixed(n) and n == 0):
                            for g in range(GROUPS):
                                add(n - 1, slot + 3, g)
                        if not (fixed(n) and n + 2 >= n_blocks(k)):
                            normalise(n + 2, slot + 2)

                    run_blocks(v, k, period)
                    last_slot = (slot0 + n_blocks(k) - 1) % 4
                    if k is not None:
                        for g in range(GROUPS):
                            add(BLOCKS - 1, last_slot, g)
                    for g in range(2):
                        v.wait_ge(y_ready[g], zcount(k, n_blocks(k), 0))
                    end = Y[last_slot % 2][:, 0:CHUNKS - 1, SB - 1, :]
                    if k is None:
                        V.tensor_copy(START[:, 1:CHUNKS, :], end).then_inc(start_set, 1)
                        V.memset(flag[:, 0:1], 1).then_inc(flag_set, 1)
                        return
                    TT(NEXT[:, 1:CHUNKS, :], end, START[:, 1:CHUNKS, :], ALU.subtract).then_inc(check_step, 1)
                    v.wait_ge(check_step, 2 * k + 1)
                    V.tensor_reduce(worst[:, 0:1], NEXT[:, 1:CHUNKS, :], AX.XY, ALU.max, apply_absolute_value=True).then_inc(check_step, 1)
                    V.tensor_copy(START[:, 1:CHUNKS, :], end).then_inc(start_set, 1)
                    v.wait_ge(worst_turned, k + 1)
                    V.tensor_reduce(worst[0:1, 1:2], psI[0][0:1, 0, :], AX.X, ALU.max).then_inc(worst_max, 1)
                    v.wait_ge(worst_max, k + 1)
                    V.tensor_scalar(flag[0:1, 0:1], worst[0:1, 1:2], START_TOL, None, ALU.is_gt).then_inc(flag_set, 1)

                sweeps(v, sweep)


_OUTS = [((16, 128, 128, 128), "float32")]


def _layouts(inputs):
    import numpy as np

    x = np.ascontiguousarray(inputs["x"])
    rows, width = x.shape[1], x.shape[2]
    a_re, a_im, b_re, b_im = [np.asarray(inputs[f"L0_conv_{n}"]) for n in ("A_real", "A_imag", "B_real", "B_imag")]
    c, k, _ = a_re.shape
    n = k * k
    t = [a.reshape(c, n).T for a in (a_re, a_im, b_re, b_im)]
    taps = np.zeros((128, 4 * c), np.float32)
    taps[0:n] = np.concatenate([t[0], t[1], t[2], t[3]], 1)
    taps[64:64 + n] = np.concatenate([t[1], t[0], t[3], t[2]], 1)
    size = width
    pad = (size - k) // 2
    u = np.arange(rows)[:, None, None]
    i, j = np.divmod(np.arange(n), k)
    v = np.arange(width)[None, None, :]
    turns = (u * (i[None, :, None] + pad) + v * (j[None, :, None] + pad)) % size
    dft = np.zeros((rows, 128, width), np.float32)
    dft[:, 0:n] = np.cos(2 * np.pi * turns / size)
    dft[:, 64:64 + n] = np.sin(2 * np.pi * turns / size)
    return {
        "x": x,
        "gate_w": np.concatenate([np.asarray(inputs[f"L0_conv_W{g}"]) for g in "fid"], 1),
        "gate_b": np.concatenate([np.asarray(inputs[f"L0_conv_b{g}"]) for g in "fid"]),
        "taps": taps,
        "dft": dft,
        "row_pick": np.eye(128, 3, dtype=np.float32),
        "ident": np.eye(128, dtype=np.float32),
        "ffn_w": np.ascontiguousarray(inputs["L0_ffn_W"]),
        "ffn_v": np.ascontiguousarray(inputs["L0_ffn_V"]),
        "gamma": np.asarray(inputs["L0_ffn_gamma"]).reshape(128, 1),
        "beta": np.asarray(inputs["L0_ffn_beta"]).reshape(128, 1),
    }


def kernel(**inputs):
    import numpy as _np
    import concourse.bacc as _bacc
    from concourse import mybir as _mybir
    from concourse.bass_utils import run_bass_kernel_spmd as _run

    nc = _bacc.Bacc("TRN2", target_bir_lowering=False, num_devices=1)
    arrays, args = {}, []
    for name, a in _layouts(inputs).items():
        a = _np.ascontiguousarray(a)
        arrays[f"in_{name}_dram"] = a
        args.append(nc.dram_tensor(f"in_{name}_dram", a.shape, _mybir.dt.from_np(a.dtype), kind="ExternalInput").ap())
    for i, (shape, dtype) in enumerate(_OUTS):
        dt = _mybir.dt.from_np(_np.dtype(dtype))
        args.append(nc.dram_tensor(f"out_{i}_dram", shape, dt, kind="ExternalOutput").ap())
    metaformer(nc, *args)
    r = _run(nc, [arrays], core_ids=[0])
    got = tuple(r.results[0][f"out_{i}_dram"] for i in range(len(_OUTS)))
    return got[0]
```

```python
from contextlib import ExitStack

import concourse.bass as bass
from concourse import mybir

F32 = mybir.dt.float32
BF16 = mybir.dt.bfloat16
I32 = mybir.dt.int32
ALU = mybir.AluOpType
ACT = mybir.ActivationFunctionType
AX = mybir.AxisListType

LN1_EPS = 1e-6
LN2_EPS = 1e-5
BN_EPS = 1e-5
SPECTRAL_EPS = 1e-8
SPECTRAL_RADIUS = 0.95

CHUNKS = 32
WARM_BLOCKS = 2
STEP_BLOCK = 8
START_TOL = 2.0 ** -19

CHAIN = [(name, part) for names, parts in (
    (["b_straight", "b_cross"], [0]), (["b_straight", "b_cross"], [1]),
    (["softplus"], [0, 1]), (["gain"], [0, 1]), (["trace1"], [0, 1]), (["det1"], [0, 1]),
    (["inp"], [0, 1]), (["a_straight", "a_cross"], [0]), (["inp"], [2, 3]), (["a_straight", "a_cross"], [1]),
    (["trace2"], [0, 1]), (["e1"], [0, 1]), (["fah"], [0, 1]), (["trace4"], [0, 1]), (["n4"], [0, 1]), (["e2"], [0, 1]),
    (["b4"], [0, 1]), (["k2"], [0, 1]), (["dk2"], [0, 1]), (["fah"], [2, 3]), (["n2"], [0, 1]), (["b4e2"], [0, 1]),
    (["b2"], [0, 1]), (["k1"], [0, 1]), (["dk1"], [0, 1]), (["n1"], [0, 1]), (["b2e1"], [0, 1]), (["b1"], [0, 1]),
    (["matrix_part", "scalar_part"], [0]), (["matrix_part", "scalar_part"], [1]),
) for name, part in ((n, p) for p in parts for n in names)]
SQUARES = ["trace1_sq", "det2", "trace1_half_sq", "trace2_sq", "det4", "trace2_half_sq", "trace4_half_sq", "scalar_coef"]


def metaformer(nc, x, gate_w, gate_b, taps, dft, row_pick, ident_in, ffn_w, ffn_v, gamma, beta, out):
    NB, ROWS, P, C = x.shape
    H = C // 2
    T = ROWS * P
    HB = NB // 2
    NGRP = NB // 4
    L = T // CHUNKS
    SB = STEP_BLOCK
    BLOCKS = L // SB
    COLS = CHUNKS * NB
    HALF = COLS // 2
    NTOK = NB * T
    TILES = CHUNKS
    assert NB * SB == P and C == P and ROWS % 2 == 0 and BLOCKS % 4 == 0 and BLOCKS >= 8 and TILES % 8 == 0

    def chain_at(r, name, part):
        return r * len(CHAIN) + (CHAIN.index((name, part)) + 1)

    def square_at(r, name, half):
        return r * (2 * len(SQUARES)) + (2 * SQUARES.index(name) + half + 1)

    x1_dram = nc.dram_tensor("x1_dram", [T, NB, C], F32, kind="Internal").ap()

    with ExitStack() as whole:
        def sem(name):
            return whole.enter_context(nc.semaphore(name))

        def keep(name, shape, dt=F32):
            return whole.enter_context(nc.sbuf_tensor(name, shape, dt))

        ident = keep("ident", [P, P])
        gram = keep("gram", [P, C + 1])
        setup_loaded = sem("setup_loaded")
        gram_copied = sem("gram_copied")
        sync_step = sem("sync_step")

        with ExitStack() as ctx:
            def sb(name, shape, dt=F32):
                return ctx.enter_context(nc.sbuf_tensor(name, shape, dt))

            def pb(name, shape):
                return ctx.enter_context(nc.psum_tensor(name, shape, F32))

            X = [sb(f"x_row{i}", [P, NB, C]) for i in range(3)]
            XN = sb("xn", [P, NB, C])
            XNT = sb("xn_t", [P, NB, P])
            FGS = [sb(f"forget{i}", [P, NB, C]) for i in range(2)]
            IGS = [sb(f"in_gate{i}", [P, NB, C]) for i in range(2)]
            SP = sb("soft", [P, NB, C])
            RL = sb("soft_relu", [P, NB, C])
            PAS = [sb(f"prod_a{i}", [P, NB, C]) for i in range(2)]
            PBuf = sb("prod_b", [P, NB, C])
            VV = sb("inp_vec", [P, NB, C])
            LNX = sb("ln_x1", [P, NB, C + 2])
            FSUM, FPROD, TR1, DT1, HS1, DT2, TR2, TR4, HS2, DT4, HS4, NN = [
                sb(n, [P, NB, H]) for n in ("forget_sum", "forget_prod", "trace1", "det1", "half1", "det2", "trace2",
                                            "trace4", "half2", "det4", "half4", "n_coef")]
            KK, AC = DT4, TR4
            stats1 = sb("stats_x", [P, NB, 6])
            stats2 = sb("stats_x1", [P, NB, 6])
            eps1, eps2, inv_c, minus_half = [sb(n, [P, NB]) for n in ("eps1", "eps2", "inv_c", "minus_half")]
            msum, mdif, vsum, rstd1, nmr1, rstd2, nmr2 = [
                sb(n, [P, NB]) for n in ("msum", "mdif", "vsum", "rstd_x", "nmr_x", "rstd_x1", "nmr_x1")]
            E = sb("dft_row", [P, P])
            taps_sb = sb("taps", [P, 4 * H])
            raw = sb("coef_raw", [P, 4 * H])
            msq = sb("mag_sq", [P, 2 * H])
            mag, mag2, sig, half_c, mag_eps, radius, minus_one = [
                sb(n, [P, H]) for n in ("mag", "mag2", "mag_sig", "half_c", "mag_eps", "radius", "minus_one")]
            coef = [sb(f"coef{i}", [P, 7, H]) for i in range(2)]
            wg = sb("gate_w", [P, 3 * C])
            bias_all = sb("bias_all", [P, 3 * C])
            bias_rest = sb("bias_rest", [P, 3 * C])
            bias_part = sb("bias_part", [P, 3 * C], BF16)
            bias_rows = sb("bias_rows", [P, 3 * C], BF16)
            pick = sb("row_pick", [P, 3])
            ones_bf = sb("ones_bf", [P, P], BF16)

            psT = pb("ps_turn", [P, 4, P])
            psG = pb("ps_gate", [P, 4, 512])
            psA = [pb(f"ps_add{i}", [P, 4, P]) for i in range(2)]
            psM = pb("ps_gram", [P, 512])

            setup = sem("setup")
            x_loaded = sem("x_loaded")
            dft_loaded = sem("dft_loaded")
            x1_stored = sem("x1_stored")
            stats1_ready = sem("stats1_ready")
            stats2_ready = sem("stats2_ready")
            norm1_step = sem("norm1_step")
            norm2_step = sem("norm2_step_x1")
            norm1_ready = sem("norm1_ready")
            norm2_ready = sem("norm2_ready")
            forget_pairs = sem("forget_pairs")
            coef_step = sem("coef_step")
            xn_ready = sem("xn_ready")
            xn_turned = sem("xn_turned")
            xnt_ready = sem("xnt_ready")
            gate_sums = sem("gate_sums")
            gate_read = sem("gate_read")
            soft_exp = sem("soft_exp")
            soft_ready = sem("soft_ready")
            chain = sem("chain")
            squares = sem("squares")
            bx_sums = sem("bx_sums")
            ah_sums = sem("ah_sums")
            x1_sums = sem("x1_sums")
            x1_copied = sem("x1_copied")
            lnx_ready = sem("lnx_ready")
            gram_added = sem("gram_added")
            coef_sums = sem("coef_sums")
            coef_raw = sem("coef_raw")
            mag_ready = sem("mag_ready")
            mag_sig = sem("mag_sig")
            coef_ready = sem("coef_ready")

            SETUP_STEPS = 9

            block = ctx.enter_context(nc.Block())

            def rows(eng, row):
                row(-1, 5)
                row(0, 0)
                row(1, 1)
                turns = (ROWS - 5) // 6
                with eng.Fori(0, turns) as i:
                    for m in range(2, 8):
                        row(6 * i + m, m % 6)
                for r in range(6 * turns + 2, ROWS + 1):
                    row(r, r % 6)

            def fixed(r):
                return isinstance(r, int)

            def from_row(r, first):
                return not fixed(r) or r >= first

            def has_next(r):
                return not fixed(r) or r + 1 < ROWS

            def has_chain(r):
                return not fixed(r) or 0 <= r < ROWS

            def has_last(r):
                return from_row(r, 1)

            def x_of(m, ahead):
                return X[(m + ahead) % 3]

            def four(buf, g):
                return buf[:, 4 * g:4 * g + 4, :]

            @block.sync
            def _(sp):
                for dst, src in ((ident[:, :], ident_in), (wg[:, :], gate_w), (taps_sb[:, :], taps),
                                 (pick[:, :], row_pick), (bias_all[:, :], gate_b.partition_broadcast(P))):
                    sp.dma_start(dst, src).then_inc(setup_loaded, 16)
                x_rows = x.rearrange("b r w c -> r w b c")
                x1_rows = x1_dram.rearrange("(r w) b c -> r w b c", w=P)

                def load(r, buf):
                    for b in (0, HB):
                        sp.dma_start(buf[:, b:b + HB, :],
                                     x_rows[bass.ds(r, 1), :, b:b + HB].rearrange("o w b c -> w (o b) c")).then_inc(x_loaded, 16)
                    sp.dma_start(E[:, :], dft[bass.ds(r, 1)].rearrange("o k w -> k (o w)")).then_inc(dft_loaded, 16)

                def row(r, m):
                    if fixed(r) and r < 0:
                        load(0, X[0])
                        sp.wait_ge(x_loaded, 32)
                        sp.wait_ge(coef_sums, 1)
                        load(1, X[1])
                        return
                    if has_last(r):
                        sp.wait_ge(x1_copied, NGRP * r)
                        sp.sem_inc(sync_step, 1)
                        sp.dma_start(x1_rows[bass.ds(r - 1, 1)].rearrange("o w b c -> w (o b) c"),
                                     x_of(m, -1)[:, :, :]).then_inc(x1_stored, 16)
                    if not fixed(r) or r + 2 < ROWS:
                        sp.wait_ge(coef_sums, r + 2)
                        sp.sem_inc(sync_step, 1)
                        if has_last(r):
                            sp.wait_ge(lnx_ready, 2 * r)
                            sp.sem_inc(sync_step, 1)
                            sp.wait_ge(x1_stored, 16 * r)
                            sp.sem_inc(sync_step, 1)
                        load(r + 2, x_of(m, 2))

                rows(sp, row)
                sp.wait_ge(x1_stored, 16 * ROWS)

            @block.tensor
            def _(pe):
                pe.wait_ge(setup, SETUP_STEPS)
                pe.wait_ge(setup_loaded, 16 * 5)

                nc.tensor.matmul(psM[:, 0:C + 1], LNX[:, 0, 0:C], LNX[:, 0, 0:C + 1], start=True, stop=False)

                def add_up(bank, g, *terms):
                    for t in terms:
                        last = nc.tensor.matmul(psA[bank][:, :, :], ident[:, :], four(t, g), start=t is terms[0], stop=t is terms[-1])
                    return last

                def row(r, m):
                    PA = PAS[m % 2]
                    if has_next(r):
                        pe.wait_ge(dft_loaded, 16 * (r + 2))
                        if from_row(r, 0):
                            pe.wait_ge(xnt_ready, NGRP * (r + 1))
                        nc.tensor.matmul(psT[:, 0:2, :], E[:, :], taps_sb[:, :], start=True, stop=True).then_inc(coef_sums, 1)
                    if has_last(r):
                        for g in range(4):
                            if g < 2:
                                pe.wait_ge(chain, chain_at(r - 1, "fah", g + 2))
                            else:
                                pe.wait_ge(x1_copied, NGRP * (r - 1) + g - 1)
                            pe.wait_ge(chain, chain_at(r - 1, "scalar_part", g // 2))
                            add_up(g % 2, g, x_of(m, -1), PAS[(m + 1) % 2], VV).then_inc(x1_sums, 1)

                    def bx(g):
                        if g >= 2:
                            pe.wait_ge(chain, chain_at(r, "inp", g - 2))
                        elif has_last(r):
                            pe.wait_ge(x1_copied, NGRP * (r - 1) + g + 3)
                        pe.wait_ge(chain, chain_at(r, "b_cross", g // 2))
                        add_up(g % 2, g, PA, PBuf).then_inc(bx_sums, 1)

                    def ah(g):
                        pe.wait_ge(chain, chain_at(r, "inp", g + 2) if g < 2 else chain_at(r, "fah", g - 2))
                        pe.wait_ge(chain, chain_at(r, "a_cross", g // 2))
                        add_up(g % 2, g, PA, PBuf).then_inc(ah_sums, 1)

                    def add_gram(half):
                        pe.wait_ge(lnx_ready, 2 * (r - 1) + half + 1)
                        for b in range(half * HB, (half + 1) * HB):
                            last = nc.tensor.matmul(psM[:, 0:C + 1], LNX[:, b, 0:C], LNX[:, b, 0:C + 1], start=False,
                                                    stop=fixed(r) and r == ROWS and b == NB - 1)
                        last.then_inc(gram_added, 1)

                    def gates(g):
                        if not has_next(r):
                            return
                        pe.wait_ge(xnt_ready, NGRP * (r + 1) + g + 1)
                        if from_row(r, 0) or g >= 1:
                            pe.wait_ge(gate_read, NGRP * (r + 1) + g)
                        for b in range(4):
                            nc.tensor.matmul(psG[:, b, 0:3 * C], ones_bf[0:32, :], bias_rows[0:32, :], start=True, stop=False)
                            last = nc.tensor.matmul(psG[:, b, 0:3 * C], XNT[:, 4 * g + b, :], wg[:, :], start=False, stop=True)
                        last.then_inc(gate_sums, 1)

                    if has_chain(r):
                        bx(0)
                        bx(1)
                    if has_next(r):
                        for g in range(NGRP):
                            pe.wait_ge(xn_ready, NGRP * (r + 1) + g + 1)
                            if g == 0:
                                pe.wait_ge(coef_raw, r + 2)
                            else:
                                pe.wait_ge(xnt_ready, NGRP * (r + 1) + g)
                            for b in range(4):
                                last = nc.tensor.transpose(psT[:, b, :], XN[:, 4 * g + b, :], ident[:, :])
                            last.then_inc(xn_turned, 1)
                            if g < 2 and has_chain(r):
                                bx(g + 2)
                            if g == 2:
                                gates(0)
                    elif has_chain(r):
                        bx(2)
                        bx(3)
                    if has_chain(r):
                        ah(0)
                        ah(1)
                        ah(2)
                        ah(3)
                    gates(1)
                    if has_last(r):
                        add_gram(0)
                    gates(2)
                    if has_last(r):
                        add_gram(1)
                    gates(3)

                rows(pe, row)

            @block.gpsimd
            def _(pool):
                NORM_STEPS, COEF_STEPS = 7, 9
                pool.wait_ge(setup, SETUP_STEPS)
                TT, TS = nc.gpsimd.tensor_tensor, nc.gpsimd.tensor_scalar

                def counted(count, base):
                    n = [0]

                    def then(ins):
                        n[0] += 1
                        ins.then_inc(count, 1)
                        pool.wait_ge(count, base + n[0])

                    return then

                def moments(then, stats, eps, rstd, nmr, free):
                    TT(msum[:, :], stats[:, :, 1], stats[:, :, 4], ALU.add)
                    TT(mdif[:, :], stats[:, :, 1], stats[:, :, 4], ALU.subtract)
                    then(TT(vsum[:, :], stats[:, :, 2], stats[:, :, 5], ALU.add))
                    then(TT(mdif[:, :], mdif[:, :], minus_half[:, :], ALU.mult))
                    TT(vsum[:, :], vsum[:, :], inv_c[:, :], ALU.mult)
                    then(TT(mdif[:, :], mdif[:, :], mdif[:, :], ALU.mult))
                    then(TT(vsum[:, :], vsum[:, :], mdif[:, :], ALU.add))
                    then(TT(vsum[:, :], vsum[:, :], eps[:, :], ALU.add))
                    free()
                    then(TT(rstd[:, :], vsum[:, :], minus_half[:, :], ALU.pow))
                    then(TT(msum[:, :], msum[:, :], minus_half[:, :], ALU.mult))
                    return TT(nmr[:, :], msum[:, :], rstd[:, :], ALU.mult)

                def row(r, m):
                    def norm_x1():
                        if not has_last(r):
                            return
                        def free2():
                            if from_row(r, 2):
                                pool.wait_ge(lnx_ready, 2 * (r - 1))

                        if has_next(r):
                            pool.wait_ge(norm1_ready, r + 2)
                        pool.wait_ge(stats2_ready, r)
                        moments(counted(norm2_step, NORM_STEPS * (r - 1)), stats2, eps2, rstd2, nmr2, free2).then_inc(norm2_ready, 1)

                    if has_chain(r):
                        FG = FGS[m % 2]
                        pool.wait_ge(gate_read, NGRP * (r + 1))
                        if from_row(r, 1):
                            pool.wait_ge(chain, chain_at(r - 1, "det1", 1))
                        TT(FSUM[:, :, :], FG[:, :, 0:H], FG[:, :, H:C], ALU.add)
                        TT(FPROD[:, :, :], FG[:, :, 0:H], FG[:, :, H:C], ALU.mult).then_inc(forget_pairs, 1)
                    if has_next(r):
                        def free1():
                            if from_row(r, 0):
                                pool.wait_ge(xn_ready, NGRP * (r + 1))

                        pool.wait_ge(stats1_ready, r + 2)
                        moments(counted(norm1_step, NORM_STEPS * (r + 1)), stats1, eps1, rstd1, nmr1, free1).then_inc(norm1_ready, 1)
                    if not has_next(r):
                        norm_x1()
                        return
                    q = coef[(m + 1) % 2]
                    then = counted(coef_step, COEF_STEPS * (r + 1))
                    pool.wait_ge(coef_raw, r + 2)
                    then(TT(msq[:, :], raw[:, 0:2 * H], raw[:, 0:2 * H], ALU.mult))
                    then(TT(mag2[:, :], msq[:, 0:H], msq[:, H:2 * H], ALU.add))
                    then(TT(mag2[:, :], mag2[:, :], mag_eps[:, :], ALU.add))
                    TT(mag[:, :], mag2[:, :], half_c[:, :], ALU.pow).then_inc(mag_ready, 1)
                    norm_x1()
                    pool.wait_ge(mag_ready, r + 2)
                    then(TT(mag2[:, :], mag[:, :], mag_eps[:, :], ALU.add))
                    then(TT(mag2[:, :], mag2[:, :], minus_one[:, :], ALU.pow))
                    pool.wait_ge(mag_sig, r + 2)
                    then(TT(mag2[:, :], mag2[:, :], sig[:, :], ALU.mult))
                    then(TT(mag2[:, :], mag2[:, :], radius[:, :], ALU.mult))
                    if from_row(r, 1):
                        pool.wait_ge(chain, chain_at(r - 1, "a_cross", 1))
                    TT(q[:, 0, :], raw[:, 0:H], mag2[:, :], ALU.mult)
                    TS(q[:, 5, :], raw[:, 3 * H:4 * H], -1.0, 0.0, ALU.mult, ALU.add)
                    TS(q[:, 4, :], raw[:, 2 * H:3 * H], 1.0, 0.0, ALU.mult, ALU.add)
                    TS(q[:, 6, :], raw[:, 3 * H:4 * H], 1.0, 0.0, ALU.mult, ALU.add)
                    then(TT(q[:, 2, :], raw[:, H:2 * H], mag2[:, :], ALU.mult))
                    TT(q[:, 1, :], q[:, 2, :], minus_one[:, :], ALU.mult)
                    TT(msq[:, 0:H], q[:, 0, :], q[:, 0, :], ALU.mult)
                    then(TT(msq[:, H:2 * H], q[:, 2, :], q[:, 2, :], ALU.mult))
                    TT(q[:, 3, :], msq[:, 0:H], msq[:, H:2 * H], ALU.add).then_inc(coef_ready, 1)

                rows(pool, row)

            @block.scalar
            def _(act):
                act.wait_ge(setup, SETUP_STEPS)

                def halves(buf, h):
                    return buf[:, h * HB:(h + 1) * HB, :]

                def row(r, m):
                    def square(name, dst, src, after, bias=0.0):
                        for h in range(2):
                            act.wait_ge(chain, chain_at(r, after, h))
                            nc.scalar.activation(halves(dst, h), halves(src, h), ACT.Square, bias=bias).then_inc(squares, 1)

                    def gates(g):
                        if not has_next(r):
                            return
                        act.wait_ge(gate_sums, NGRP * (r + 1) + g + 1)
                        if g == 0 and has_last(r):
                            act.wait_ge(forget_pairs, r)
                        nc.scalar.activation(four(FGS[(m + 1) % 2], g), psG[:, :, 0:C], ACT.Sigmoid)
                        nc.scalar.activation(four(IGS[(m + 1) % 2], g), psG[:, :, C:2 * C], ACT.Sigmoid)
                        nc.scalar.activation(four(RL, g), psG[:, :, 2 * C:3 * C], ACT.Relu)
                        nc.scalar.activation(four(SP, g), psG[:, :, 2 * C:3 * C], ACT.Abs).then_inc(gate_read, 1)

                    def xn(g):
                        for b in range(4 * g, 4 * g + 4):
                            last = nc.scalar.activation(XN[:, b, :], x_of(m, 1)[:, b, :], ACT.Identity,
                                                        bias=nmr1[:, b:b + 1], scale=rstd1[:, b:b + 1])
                        last.then_inc(xn_ready, 1)

                    def lnx(first):
                        for b in range(first, first + HB):
                            last = nc.scalar.activation(LNX[:, b, 0:C], x_of(m, -1)[:, b, :], ACT.Identity,
                                                        bias=nmr2[:, b:b + 1], scale=rstd2[:, b:b + 1])
                        last.then_inc(lnx_ready, 1)

                    def xnt(g):
                        act.wait_ge(xn_turned, NGRP * (r + 1) + g + 1)
                        nc.scalar.activation(four(XNT, g), psT[:, :, :], ACT.Identity).then_inc(xnt_ready, 1)

                    if has_next(r):
                        act.wait_ge(coef_sums, r + 2)
                        if from_row(r, 0):
                            act.wait_ge(coef_ready, r + 1)
                        nc.scalar.activation(raw[:, :], psT[:, 0:2, :].rearrange("p a b -> p (a b)"), ACT.Identity).then_inc(coef_raw, 1)
                    if has_last(r):
                        for g in range(NGRP):
                            act.wait_ge(x1_sums, NGRP * (r - 1) + g + 1)
                            nc.scalar.activation(four(x_of(m, -1), g), psA[g % 2][:, :, :], ACT.Identity).then_inc(x1_copied, 1)
                    if has_next(r):
                        act.wait_ge(norm1_ready, r + 2)
                        if from_row(r, 0):
                            act.wait_ge(chain, chain_at(r, "b_cross", 1))
                        xn(0)
                        xn(1)
                        xnt(0)
                        xn(2)
                        xnt(1)
                    if has_chain(r):
                        square("trace1_sq", TR2, TR1, "trace1")
                        square("det2", DT2, DT1, "det1")
                    if has_next(r):
                        xn(3)
                        xnt(2)
                        xnt(3)
                    if has_chain(r):
                        square("trace1_half_sq", HS1, TR1, "trace1", 0.5)
                        square("trace2_sq", TR4, TR2, "trace2")
                        square("det4", DT4, DT2, "trace2")
                    gates(0)
                    if has_chain(r):
                        square("trace2_half_sq", HS2, TR2, "trace2", 0.5)
                        square("trace4_half_sq", HS4, TR4, "trace4", 0.5)
                    if has_next(r):
                        act.wait_ge(mag_ready, r + 2)
                        nc.scalar.activation(sig[:, :], mag[:, :], ACT.Sigmoid).then_inc(mag_sig, 1)
                    if has_last(r):
                        act.wait_ge(norm2_ready, r)
                        if from_row(r, 2):
                            act.wait_ge(gram_added, 2 * (r - 1))
                        lnx(0)
                    gates(1)
                    if has_last(r):
                        lnx(HB)
                    gates(2)
                    if has_chain(r):
                        for h in range(2):
                            act.wait_ge(chain, chain_at(r, "n1", h))
                            nc.scalar.activation(halves(AC, h), halves(NN, h), ACT.Identity, scale=-1.0, bias=1.0).then_inc(squares, 1)
                    gates(3)
                    if has_next(r):
                        act.wait_ge(gate_read, NGRP * (r + 2))
                        for h in range(2):
                            nc.scalar.activation(halves(SP, h), halves(SP, h), ACT.Exp, scale=-1.0).then_inc(soft_exp, 1)
                        for h in range(2):
                            act.wait_ge(soft_exp, 2 * (r + 1) + h + 1)
                            nc.scalar.activation(halves(SP, h), halves(SP, h), ACT.Ln, bias=1.0).then_inc(soft_ready, 1)

                rows(act, row)

            @block.vector
            def _(v):
                done = [0]

                def step(ins):
                    done[0] += 1
                    ins.then_inc(setup, 1)
                    v.wait_ge(setup, done[0])

                V = nc.vector
                V.memset(eps1[:, :], LN1_EPS)
                V.memset(eps2[:, :], LN2_EPS)
                V.memset(minus_half[:, :], -0.5)
                V.memset(half_c[:, :], 0.5)
                V.memset(inv_c[:, :], 1.0 / C)
                V.memset(mag_eps[:, :], SPECTRAL_EPS)
                V.memset(radius[:, :], SPECTRAL_RADIUS)
                V.memset(minus_one[:, :], -1.0)
                V.memset(ones_bf[:, :], 1.0)
                step(V.memset(LNX[:, :, :], 0.0))
                v.wait_ge(setup_loaded, 16 * 5)
                V.tensor_scalar(taps_sb[64:P, H:2 * H], taps_sb[64:P, H:2 * H], -1.0, None, ALU.mult)
                V.tensor_scalar(taps_sb[64:P, 3 * H:4 * H], taps_sb[64:P, 3 * H:4 * H], -1.0, None, ALU.mult)
                V.memset(LNX[:, :, C:C + 1], 1.0)
                step(V.tensor_scalar(bias_all[:, 0:C], bias_all[:, 0:C], 2.0, None, ALU.add))
                step(V.tensor_copy(bias_part[:, :], bias_all[:, :]))
                V.tensor_tensor(bias_rest[:, :], bias_all[:, :], bias_part[:, :], ALU.subtract)
                step(V.tensor_scalar(bias_rows[:, :], bias_part[:, :], pick[:, 0:1], None, ALU.mult))
                step(V.tensor_copy(bias_part[:, :], bias_rest[:, :]))
                step(V.tensor_tensor(bias_rest[:, :], bias_rest[:, :], bias_part[:, :], ALU.subtract))
                step(V.scalar_tensor_tensor(bias_rows[:, :], bias_part[:, :], pick[:, 1:2], bias_rows[:, :], ALU.mult, ALU.add))
                step(V.tensor_copy(bias_part[:, :], bias_rest[:, :]))
                step(V.scalar_tensor_tensor(bias_rows[:, :], bias_part[:, :], pick[:, 2:3], bias_rows[:, :], ALU.mult, ALU.add))

                def full(buf, h):
                    return buf[:, h * HB:(h + 1) * HB, :].rearrange("p b (k c) -> p b k c", k=2)

                def crossed(buf, h):
                    return full(buf, h)[:, :, ::-1, :]

                def pair(buf, h):
                    return buf[:, h * HB:(h + 1) * HB, :]

                def both(buf, h):
                    return pair(buf, h).unsqueeze(2).broadcast_to([P, HB, 2, H])

                STT, TT = V.scalar_tensor_tensor, V.tensor_tensor
                M, A, S = ALU.mult, ALU.add, ALU.subtract

                def row(r, m):
                    q, FG, IG, PA = coef[m % 2], FGS[m % 2], IGS[m % 2], PAS[m % 2]
                    order = iter(CHAIN)

                    def cf(k):
                        return q[:, k, :].unsqueeze(1).broadcast_to([P, HB, H])

                    def cf2(k, same):
                        a = q[:, k:k + 1, :].broadcast_to([P, 2, H]) if same else q[:, k:k + 2, :]
                        return a.unsqueeze(1).broadcast_to([P, HB, 2, H])

                    def at(name, make, parts=(0, 1), needs=None, square=None, sums=None):
                        for p in parts:
                            assert next(order) == (name, p)
                            if needs:
                                v.wait_ge(chain, chain_at(r, needs, p // 2 if sums else p))
                            if square:
                                v.wait_ge(squares, square_at(r, square, p))
                            if sums:
                                v.wait_ge(sums, NGRP * r + p + 1)
                            make(p).then_inc(chain, 1)

                    if has_chain(r):
                        v.wait_ge(coef_ready, r + 1)
                        v.wait_ge(xn_ready, NGRP * (r + 1))
                        for h in range(2):
                            at("b_straight", lambda h: TT(full(PA, h), full(XN, h), cf2(4, True), M), [h])
                            at("b_cross", lambda h: TT(full(PBuf, h), crossed(XN, h), cf2(5, False), M), [h])
                    if has_next(r):
                        v.wait_ge(x_loaded, 32 * (r + 2))
                        if from_row(r, 0):
                            v.wait_ge(norm1_ready, r + 1)
                        for b in range(NB):
                            last = V.bn_stats(stats1[:, b, :], x_of(m, 1)[:, b, :])
                        last.then_inc(stats1_ready, 1)
                    if has_chain(r):
                        v.wait_ge(soft_ready, 2 * r + 2)
                        at("softplus", lambda h: TT(full(SP, h), full(SP, h), full(RL, h), A))
                        at("gain", lambda h: STT(full(IG, h), full(SP, h), 0.1, full(IG, h), M, M), needs="softplus")
                        v.wait_ge(forget_pairs, r + 1)
                        at("trace1", lambda h: TT(pair(TR1, h), pair(FSUM, h), cf(0), M))
                        at("det1", lambda h: TT(pair(DT1, h), pair(FPROD, h), cf(3), M))
                    inp = lambda g: TT(four(VV, g), psA[g % 2][:, :, :], four(IG, g), M)
                    fah = lambda g: TT(four(PA, g), psA[g % 2][:, :, :], four(FG, g), M)
                    a_straight = lambda h: TT(full(PA, h), full(VV, h), cf2(0, True), M)
                    a_cross = lambda h: TT(full(PBuf, h), crossed(VV, h), cf2(1, False), M)
                    if has_chain(r):
                        at("inp", inp, [0, 1], needs="gain", sums=bx_sums)
                        v.wait_ge(chain, chain_at(r, "inp", 1))
                        at("a_straight", a_straight, [0])
                        at("a_cross", a_cross, [0])
                    if has_last(r):
                        v.wait_ge(x1_copied, NGRP * r)
                        if from_row(r, 2):
                            v.wait_ge(norm2_ready, r - 1)
                        for b in range(NB):
                            last = V.bn_stats(stats2[:, b, :], x_of(m, -1)[:, b, :])
                        last.then_inc(stats2_ready, 1)
                    if not has_chain(r):
                        return
                    at("inp", inp, [2, 3], needs="gain", sums=bx_sums)
                    v.wait_ge(chain, chain_at(r, "inp", 3))
                    at("a_straight", a_straight, [1])
                    at("a_cross", a_cross, [1])
                    at("trace2", lambda h: STT(pair(TR2, h), pair(DT1, h), -2.0, pair(TR2, h), M, A), square="det2")
                    at("e1", lambda h: STT(pair(HS1, h), pair(HS1, h), -0.25, pair(DT1, h), A, S), square="trace1_half_sq")
                    at("fah", fah, [0, 1], sums=ah_sums)
                    at("trace4", lambda h: STT(pair(TR4, h), pair(DT2, h), -2.0, pair(TR4, h), M, A), square="trace2_sq")
                    at("n4", lambda h: STT(pair(NN, h), pair(TR4, h), 1.0, pair(DT4, h), A, M), needs="trace4", square="det4")
                    at("e2", lambda h: STT(pair(HS2, h), pair(HS2, h), -0.25, pair(DT2, h), A, S), square="trace2_half_sq")
                    at("b4", lambda h: STT(pair(HS4, h), pair(HS4, h), 0.75, pair(DT4, h), A, S), square="trace4_half_sq")
                    at("k2", lambda h: STT(pair(KK, h), pair(TR2, h), 1.0, pair(HS4, h), A, M), needs="b4")
                    at("dk2", lambda h: TT(pair(KK, h), pair(KK, h), pair(DT2, h), M), needs="k2")
                    at("fah", fah, [2, 3], sums=ah_sums)
                    at("n2", lambda h: TT(pair(KK, h), pair(KK, h), pair(NN, h), A), needs="dk2")
                    at("b4e2", lambda h: TT(pair(HS4, h), pair(HS4, h), pair(HS2, h), M))
                    at("b2", lambda h: STT(pair(HS2, h), pair(HS4, h), 1.0, pair(NN, h), A, S), needs="b4e2")
                    at("k1", lambda h: STT(pair(NN, h), pair(TR1, h), 1.0, pair(HS2, h), A, M), needs="b2")
                    at("dk1", lambda h: TT(pair(NN, h), pair(NN, h), pair(DT1, h), M), needs="k1")
                    at("n1", lambda h: TT(pair(NN, h), pair(NN, h), pair(KK, h), A), needs="dk1")
                    at("b2e1", lambda h: TT(pair(HS2, h), pair(HS2, h), pair(HS1, h), M))
                    at("b1", lambda h: STT(pair(HS2, h), pair(HS2, h), 1.0, pair(KK, h), A, S), needs="b2e1")
                    for h in range(2):
                        at("matrix_part", lambda h: TT(full(PA, h), full(PA, h), both(HS2, h), M), [h], needs="b1")
                        at("scalar_part", lambda h: TT(full(VV, h), full(VV, h), both(AC, h), M), [h], square="scalar_coef")

                rows(v, row)
                v.wait_ge(gram_added, 2 * ROWS)
                V.tensor_copy(gram[:, :], psM[:, 0:C + 1]).then_inc(gram_copied, 1)

        with ExitStack() as ctx:
            def sb(name, shape, dt=F32):
                return ctx.enter_context(nc.sbuf_tensor(name, shape, dt))

            def pb(name, shape):
                return ctx.enter_context(nc.psum_tensor(name, shape, F32))

            XT = [sb(f"x1_block{i}", [P, TILES, C]) for i in range(4)]
            OUT = [sb(f"out_half{i}", [P, TILES // 2, C]) for i in range(2)]
            LN = sb("ln_block", [P, TILES, C])
            LNT = [sb(f"ln_t{i}", [P, CHUNKS, SB, NB]) for i in range(2)]
            Y = [sb(f"y_t{i}", [P, CHUNKS, SB, NB]) for i in range(2)]
            START = sb("start", [P, CHUNKS, NB])
            NEXT = sb("next_start", [P, CHUNKS, NB])
            stats = sb("stats_block", [P, TILES, 6])
            eps = sb("eps_wide", [P, TILES])
            inv_c = sb("inv_c2", [P, TILES])
            minus_half = sb("minus_half2", [P, TILES])
            msum, mdif, vsum, rstd, nmr = [sb(n + "2", [P, TILES]) for n in ("msum", "mdif", "vsum", "rstd", "nmr")]
            w_sb, v_sb, w_t, v_t, prod, ws_t = [sb(n, [P, C]) for n in ("w_sb", "v_sb", "w_t", "v_t", "prod", "ws_t")]
            vec = sb("vec", [P, 16])
            ones = sb("ones", [P, 1])
            worst = sb("worst", [P, 2])
            flag = sb("flag", [1, 2], I32)

            psZ = [[pb(f"ps_z{g}{i}", [P, 512]) for i in range(2)] for g in range(2)]
            psI = [pb(f"ps_in{i}", [P, 4, P]) for i in range(2)]
            psO = [pb(f"ps_out{i}", [P, 4, P]) for i in range(2)]
            LOADED = 16 * (CHUNKS // 8)
            GROUPS = TILES // 4

            loaded2 = sem("loaded2")
            fold = sem("fold")
            fold_pe = sem("fold_pe")
            fold_pool = sem("fold_pool")
            x_block = sem("x_block")
            stats2 = sem("stats2")
            norm2_step = sem("norm2_step")
            norm2 = sem("norm2")
            ln_block = sem("ln_block")
            ln_turned = sem("ln_turned")
            lnt_copied = sem("lnt_copied")
            z_ready = [sem(f"z_ready{g}") for g in range(2)]
            y_ready = [sem(f"y_ready{g}") for g in range(2)]
            y_turned = sem("y_turned")
            added = sem("added")
            out_stored = [sem(f"out_stored{h}") for h in range(2)]
            start_set = sem("start_set")
            check_step = sem("check_step")
            worst_max = sem("worst_max")
            worst_turned = sem("worst_turned")
            flag_set = sem("flag_set")
            verdict_seen = sem("verdict_seen")

            blocks_v = x1_dram.rearrange("(j n t) b c -> n (t b) j c", n=BLOCKS, t=SB)
            out_v = out.rearrange("b r w c -> b (r w) c").rearrange("b (j n t) c -> n t b j c", n=BLOCKS, t=SB)
            FOLD_TURNED, FOLD_PROD, FOLD_VAR, FOLD_SCALED, FOLD_STEPS = 3, 4, 8, 12, 13
            SWEEPS = CHUNKS

            block = ctx.enter_context(nc.Block())

            def q_of(k, n):
                return n if k is None else WARM_BLOCKS + k * BLOCKS + n

            def n_blocks(k):
                return WARM_BLOCKS if k is None else BLOCKS

            def run_blocks(eng, k, body):
                if k is None:
                    for n in range(WARM_BLOCKS):
                        body(n, n % 4)
                    return
                for n in range(4):
                    body(n, (n + WARM_BLOCKS) % 4)
                if BLOCKS > 8:
                    with eng.Fori(1, BLOCKS // 4 - 1) as i:
                        for m in range(4):
                            body(4 * i + m, (m + WARM_BLOCKS) % 4)
                for n in range(BLOCKS - 4, BLOCKS):
                    body(n, (n + WARM_BLOCKS) % 4)

            def sweeps(eng, sweep):
                sweep(None)
                eng.wait_ge(flag_set, 1)
                with eng.Fori(0, SWEEPS) as k:
                    again = eng.value_load(flag[0:1, 0:1], min_val=0, max_val=1)
                    with eng.If(again == 1):
                        sweep(k)
                        eng.wait_ge(flag_set, k + 2)
                        eng.sem_inc(verdict_seen, 1)

            def fixed(n):
                return isinstance(n, int)

            def chunks(g):
                return slice(g * CHUNKS // 2, (g + 1) * CHUNKS // 2)

            @block.sync
            def _(sp):
                sp.dma_start(w_sb[:, :], ffn_w).then_inc(loaded2, 16)
                sp.dma_start(v_sb[:, :], ffn_v).then_inc(loaded2, 16)
                sp.dma_start(vec[:, 0:1], gamma).then_inc(loaded2, 16)
                sp.dma_start(vec[:, 1:2], beta).then_inc(loaded2, 16)

                def sweep(k):
                    def load(n, slot):
                        src = n + (BLOCKS - WARM_BLOCKS) if k is None else n
                        if not (k is None and n == 0):
                            sp.wait_ge(x_block, LOADED * q_of(k, n))
                            sp.sem_inc(sync_step, 1)
                        for j in range(0, CHUNKS, 8):
                            sp.dma_start(XT[slot % 4][:, j:j + 8, :],
                                         blocks_v[bass.ds(src, 1), :, j:j + 8].rearrange("o p j c -> p (o j) c")).then_inc(x_block, 16)

                    if k is None:
                        for n in range(WARM_BLOCKS):
                            load(n, n)
                        return
                    for n in range(4):
                        if n == 0:
                            sp.wait_ge(ln_block, q_of(k, 0))
                            sp.sem_inc(sync_step, 1)
                        load(n, n + WARM_BLOCKS)

                    def store(n, slot):
                        for h in range(2):
                            sp.wait_ge(added, GROUPS * (k * BLOCKS + n) + GROUPS // 2 * (h + 1))
                            sp.sem_inc(sync_step, 1)
                            js = slice(h * TILES // 2, (h + 1) * TILES // 2)
                            for t in range(SB):
                                sp.dma_start(out_v[bass.ds(n, 1), t, :, js, :].rearrange("o b j c -> (o b) j c"),
                                             OUT[h][t * NB:(t + 1) * NB, :, :]).then_inc(out_stored[h], 16)
                        if not (fixed(n) and n + 4 >= BLOCKS):
                            load(n + 4, slot)

                    run_blocks(sp, k, store)
                    for h in range(2):
                        sp.wait_ge(out_stored[h], 16 * SB * BLOCKS * (k + 1))
                        sp.sem_inc(sync_step, 1)

                sp.wait_ge(gram_copied, 1)
                sweeps(sp, sweep)

            @block.gpsimd
            def _(pool):
                TT, TS = nc.gpsimd.tensor_tensor, nc.gpsimd.tensor_scalar
                pool.wait_ge(fold, FOLD_VAR)
                TT(vec[:, 6:7], vec[:, 5:6], minus_half[:, 0:1], ALU.pow).then_inc(fold_pool, 1)

                def sweep(k):
                    def norm(n, slot):
                        q = q_of(k, n)
                        m = [0]

                        def then(ins):
                            m[0] += 1
                            ins.then_inc(norm2_step, 1)
                            pool.wait_ge(norm2_step, 7 * q + m[0])

                        pool.wait_ge(stats2, q + 1)
                        TT(msum[:, :], stats[:, :, 1], stats[:, :, 4], ALU.add)
                        TT(mdif[:, :], stats[:, :, 1], stats[:, :, 4], ALU.subtract)
                        then(TT(vsum[:, :], stats[:, :, 2], stats[:, :, 5], ALU.add))
                        then(TT(mdif[:, :], mdif[:, :], minus_half[:, :], ALU.mult))
                        TT(vsum[:, :], vsum[:, :], inv_c[:, :], ALU.mult)
                        then(TT(mdif[:, :], mdif[:, :], mdif[:, :], ALU.mult))
                        then(TT(vsum[:, :], vsum[:, :], mdif[:, :], ALU.add))
                        then(TT(vsum[:, :], vsum[:, :], eps[:, :], ALU.add))
                        if not (k is None and n == 0):
                            pool.wait_ge(ln_block, q)
                        then(TT(rstd[:, :], vsum[:, :], minus_half[:, :], ALU.pow))
                        then(TT(msum[:, :], msum[:, :], minus_half[:, :], ALU.mult))
                        TT(nmr[:, :], msum[:, :], rstd[:, :], ALU.mult).then_inc(norm2, 1)

                    run_blocks(pool, k, norm)

                sweeps(pool, sweep)

            def per_step(total, steps):
                return [total * (t + 1) // steps - total * t // steps if t < steps else 0 for t in range(SB)]

            IN_AT = per_step(GROUPS, 6)
            OUT_AT = per_step(GROUPS, 8)

            def zcount(k, n, t):
                return SB * q_of(k, n) + t

            def prev(k, n):
                return None if fixed(n) and n == 0 else n - 1

            @block.tensor
            def _(pe):
                pe.wait_ge(loaded2, 64)
                pe.wait_ge(gram_copied, 1)
                nc.tensor.transpose(psI[0][:, 0, :], w_sb[:, :], ident[:, :]).then_inc(fold_pe, 1)
                nc.tensor.transpose(psI[1][:, 1, :], v_sb[:, :], ident[:, :]).then_inc(fold_pe, 1)
                pe.wait_ge(fold, FOLD_TURNED)
                nc.tensor.matmul(psO[0][:, 0, 0:C], gram[:, 0:C], w_t[:, :], start=True, stop=True).then_inc(fold_pe, 1)
                nc.tensor.matmul(psO[1][:, 0, 0:1], w_t[:, :], gram[:, C:C + 1], start=True, stop=True).then_inc(fold_pe, 1)
                pe.wait_ge(fold, FOLD_PROD)
                nc.tensor.matmul(psI[1][:, 0, 0:1], prod[:, :], ones[:, :], start=True, stop=True).then_inc(fold_pe, 1)
                pe.wait_ge(fold, FOLD_SCALED)
                nc.tensor.transpose(psI[0][:, 0, :], prod[:, :], ident[:, :]).then_inc(fold_pe, 1)
                pe.wait_ge(fold, FOLD_STEPS)

                def turn_in(k, n, slot, g):
                    at = GROUPS * q_of(k, n) + g
                    if g == 0:
                        pe.wait_ge(ln_block, q_of(k, n) + 1)
                    if not (k is None and n == 0 and g < 2):
                        pe.wait_ge(lnt_copied, at - 1)
                    for j in range(4):
                        last = nc.tensor.transpose(psI[g % 2][:, j, :], LN[:, 4 * g + j, :], ident[:, :])
                    last.then_inc(ln_turned, 1)

                def turn_out(k, n, slot, g):
                    at = GROUPS * (k * BLOCKS + n) + g
                    if not (fixed(n) and n == 0 and g < 2):
                        pe.wait_ge(added, at - 1)
                    for j in range(4):
                        last = nc.tensor.transpose(psO[g % 2][:, j, :], Y[slot % 2][:, 4 * g + j].rearrange("p t b -> p (t b)"), ident[:, :])
                    last.then_inc(y_turned, 1)

                def input_part(n_slot, g, t, stop=False):
                    nc.tensor.matmul(psZ[g][t % 2][:, 0:HALF], ws_t[:, :], LNT[n_slot % 2][:, chunks(g), t, :], start=True, stop=False)

                def sweep(k):
                    if k is None:
                        pe.wait_ge(start_set, 1)
                    slot0 = 0 if k is None else WARM_BLOCKS % 4
                    for g in range(GROUPS):
                        turn_in(k, 0, slot0, g)
                    pe.wait_ge(lnt_copied, GROUPS * (q_of(k, 0) + 1))
                    for g in range(2):
                        input_part(slot0, g, 0)

                    def steps(n, slot):
                        is_last = fixed(n) and n == n_blocks(k) - 1
                        is_first = fixed(n) and n == 0
                        gi = go = 0
                        for t in range(SB):
                            for g in range(2):
                                if t == 0 and is_first:
                                    rhs = START[:, chunks(g), :]
                                    if k is not None:
                                        pe.wait_ge(start_set, k + 2)
                                else:
                                    pe.wait_ge(y_ready[g], zcount(k, n, t))
                                    src = Y[slot % 2] if t else Y[(slot + 1) % 2]
                                    rhs = src[:, chunks(g), (t - 1) % SB, :]
                                nc.tensor.matmul(psZ[g][t % 2][:, 0:HALF], v_t[:, :], rhs, start=False, stop=True).then_inc(z_ready[g], 1)
                                if t + 1 < SB:
                                    input_part(slot, g, t + 1)
                                elif not is_last:
                                    if g == 0:
                                        pe.wait_ge(lnt_copied, GROUPS * (q_of(k, n) + 2))
                                    input_part(slot + 1, g, 0)
                                if g == 0 and not is_last:
                                    for _ in range(IN_AT[t]):
                                        turn_in(k, n + 1, slot + 1, gi)
                                        gi += 1
                                if g == 1 and not is_first and k is not None:
                                    for _ in range(OUT_AT[t]):
                                        turn_out(k, n - 1, slot + 3, go)
                                        go += 1
                        if is_last and k is not None:
                            pe.wait_ge(y_ready[0], zcount(k, n, SB))
                            pe.wait_ge(y_ready[1], zcount(k, n, SB))
                            for g in range(GROUPS):
                                turn_out(k, n, slot, g)

                    run_blocks(pe, k, steps)
                    if k is not None:
                        pe.wait_ge(check_step, 2 * (k + 1))
                        nc.tensor.transpose(psI[0][0:1, 0, :], worst[:, 0:1], ident[:, :]).then_inc(worst_turned, 1)

                sweeps(pe, sweep)

            @block.scalar
            def _(act):
                act.wait_ge(fold, FOLD_STEPS)

                def copy_in(k, n, slot, g):
                    at = GROUPS * q_of(k, n) + g
                    act.wait_ge(ln_turned, at + 1)
                    nc.scalar.activation(LNT[slot % 2][:, 4 * g:4 * g + 4].rearrange("p j t b -> p j (t b)"), psI[g % 2][:, :, :],
                                         ACT.Identity).then_inc(lnt_copied, 1)

                def sweep(k):
                    slot0 = 0 if k is None else WARM_BLOCKS % 4
                    for g in range(GROUPS):
                        copy_in(k, 0, slot0, g)

                    def steps(n, slot):
                        is_last = fixed(n) and n == n_blocks(k) - 1
                        is_first = fixed(n) and n == 0
                        gi = 0
                        if k is not None and not (fixed(n) and n < 2):
                            act.wait_ge(y_turned, GROUPS * (k * BLOCKS + n - 1))
                        elif k is not None and is_first:
                            act.wait_ge(start_set, k + 2)
                        for t in range(SB):
                            for g in range(2):
                                act.wait_ge(z_ready[g], zcount(k, n, t) + 1)
                                nc.scalar.activation(Y[slot % 2][:, chunks(g), t, :], psZ[g][t % 2][:, 0:HALF].rearrange("p (j b) -> p j b", b=NB),
                                                     ACT.Sigmoid, bias=vec[:, 9:10]).then_inc(y_ready[g], 1)
                                if g == 0 and not is_last:
                                    for _ in range(IN_AT[t]):
                                        copy_in(k, n + 1, slot + 1, gi)
                                        gi += 1

                    run_blocks(act, k, steps)

                sweeps(act, sweep)

            @block.vector
            def _(v):
                V = nc.vector
                TT, STT = V.tensor_tensor, V.scalar_tensor_tensor
                done = [0]

                def step(ins):
                    done[0] += 1
                    ins.then_inc(fold, 1)
                    v.wait_ge(fold, done[0])
                    return done[0]

                V.memset(eps[:, :], LN2_EPS)
                V.memset(inv_c[:, :], 1.0 / C)
                V.memset(minus_half[:, :], -0.5)
                V.memset(ones[:, :], 1.0)
                V.memset(START[:, :, :], 0.0).then_inc(start_set, 1)
                step(V.memset(NEXT[:, :, :], 0.0))
                v.wait_ge(loaded2, 64)
                v.wait_ge(fold_pe, 1)
                step(V.tensor_copy(w_t[:, :], psI[0][:, 0, :]))
                v.wait_ge(fold_pe, 2)
                assert step(V.tensor_copy(v_t[:, :], psI[1][:, 1, :])) == FOLD_TURNED
                v.wait_ge(fold_pe, 3)
                assert step(TT(prod[:, :], psO[0][:, 0, 0:C], w_t[:, :], ALU.mult)) == FOLD_PROD
                v.wait_ge(fold_pe, 4)
                step(V.tensor_scalar(vec[:, 3:4], psO[1][:, 0, 0:1], 1.0 / NTOK, None, ALU.mult))
                step(TT(vec[:, 4:5], vec[:, 3:4], vec[:, 3:4], ALU.mult))
                v.wait_ge(fold_pe, 5)
                step(STT(vec[:, 5:6], psI[1][:, 0, 0:1], 1.0 / NTOK, vec[:, 4:5], ALU.mult, ALU.subtract))
                assert step(V.tensor_scalar(vec[:, 5:6], vec[:, 5:6], 0.0, BN_EPS, ALU.max, ALU.add)) == FOLD_VAR
                v.wait_ge(fold_pool, 1)
                step(TT(vec[:, 7:8], vec[:, 6:7], vec[:, 0:1], ALU.mult))
                step(TT(vec[:, 8:9], vec[:, 3:4], vec[:, 7:8], ALU.mult))
                step(TT(vec[:, 9:10], vec[:, 1:2], vec[:, 8:9], ALU.subtract))
                assert step(V.tensor_scalar(prod[:, :], w_sb[:, :], vec[:, 7:8], None, ALU.mult)) == FOLD_SCALED
                v.wait_ge(fold_pe, 6)
                assert step(V.tensor_copy(ws_t[:, :], psI[0][:, 0, :])) == FOLD_STEPS

                def sweep(k):
                    def statistics(n, slot):
                        q = q_of(k, n)
                        v.wait_ge(x_block, LOADED * (q + 1))
                        if not (k is None and n == 0):
                            v.wait_ge(norm2, q)
                        for j in range(TILES):
                            last = V.bn_stats(stats[:, j, :], XT[slot % 4][:, j, :])
                        last.then_inc(stats2, 1)

                    def normalise(n, slot):
                        q = q_of(k, n)
                        v.wait_ge(norm2, q + 1)
                        if not (k is None and n == 0):
                            v.wait_ge(ln_turned, GROUPS * q)
                        for j in range(TILES):
                            last = V.tensor_scalar(LN[:, j, :], XT[slot % 4][:, j, :], rstd[:, j:j + 1], nmr[:, j:j + 1], ALU.mult, ALU.add)
                        last.then_inc(ln_block, 1)

                    def add(n, slot, g):
                        at = GROUPS * (k * BLOCKS + n) + g
                        half = (2 * g) // GROUPS
                        v.wait_ge(y_turned, at + 1)
                        if g == half * (GROUPS // 2) and not (fixed(n) and n == 0):
                            v.wait_ge(out_stored[half], 16 * SB * (k * BLOCKS + n))
                        o = OUT[half][:, (4 * g) % (TILES // 2):(4 * g) % (TILES // 2) + 4, :]
                        TT(o, XT[slot % 4][:, 4 * g:4 * g + 4, :], psO[g % 2][:, :, :], ALU.add).then_inc(added, 1)

                    slot0 = 0 if k is None else WARM_BLOCKS % 4
                    statistics(0, slot0)
                    normalise(0, slot0)
                    statistics(1, slot0 + 1)
                    normalise(1, slot0 + 1)

                    def period(n, slot):
                        if not (fixed(n) and n + 2 >= n_blocks(k)):
                            statistics(n + 2, slot + 2)
                        if k is not None and not (fixed(n) and n == 0):
                            for g in range(GROUPS):
                                add(n - 1, slot + 3, g)
                        if not (fixed(n) and n + 2 >= n_blocks(k)):
                            normalise(n + 2, slot + 2)

                    run_blocks(v, k, period)
                    last_slot = (slot0 + n_blocks(k) - 1) % 4
                    if k is not None:
                        for g in range(GROUPS):
                            add(BLOCKS - 1, last_slot, g)
                    for g in range(2):
                        v.wait_ge(y_ready[g], zcount(k, n_blocks(k), 0))
                    end = Y[last_slot % 2][:, 0:CHUNKS - 1, SB - 1, :]
                    if k is None:
                        V.tensor_copy(START[:, 1:CHUNKS, :], end).then_inc(start_set, 1)
                        V.memset(flag[:, 0:1], 1).then_inc(flag_set, 1)
                        return
                    TT(NEXT[:, 1:CHUNKS, :], end, START[:, 1:CHUNKS, :], ALU.subtract).then_inc(check_step, 1)
                    v.wait_ge(check_step, 2 * k + 1)
                    V.tensor_reduce(worst[:, 0:1], NEXT[:, 1:CHUNKS, :], AX.XY, ALU.max, apply_absolute_value=True).then_inc(check_step, 1)
                    V.tensor_copy(START[:, 1:CHUNKS, :], end).then_inc(start_set, 1)
                    v.wait_ge(worst_turned, k + 1)
                    V.tensor_reduce(worst[0:1, 1:2], psI[0][0:1, 0, :], AX.X, ALU.max).then_inc(worst_max, 1)
                    v.wait_ge(worst_max, k + 1)
                    V.tensor_scalar(flag[0:1, 0:1], worst[0:1, 1:2], START_TOL, None, ALU.is_gt).then_inc(flag_set, 1)

                sweeps(v, sweep)


_OUTS = [((16, 128, 128, 128), "float32")]


def _layouts(inputs):
    import numpy as np

    x = np.ascontiguousarray(inputs["x"])
    rows, width = x.shape[1], x.shape[2]
    a_re, a_im, b_re, b_im = [np.asarray(inputs[f"L0_conv_{n}"]) for n in ("A_real", "A_imag", "B_real", "B_imag")]
    c, k, _ = a_re.shape
    n = k * k
    t = [a.reshape(c, n).T for a in (a_re, a_im, b_re, b_im)]
    taps = np.zeros((128, 4 * c), np.float32)
    taps[0:n] = np.concatenate([t[0], t[1], t[2], t[3]], 1)
    taps[64:64 + n] = np.concatenate([t[1], t[0], t[3], t[2]], 1)
    size = width
    pad = (size - k) // 2
    u = np.arange(rows)[:, None, None]
    i, j = np.divmod(np.arange(n), k)
    v = np.arange(width)[None, None, :]
    turns = (u * (i[None, :, None] + pad) + v * (j[None, :, None] + pad)) % size
    dft = np.zeros((rows, 128, width), np.float32)
    dft[:, 0:n] = np.cos(2 * np.pi * turns / size)
    dft[:, 64:64 + n] = np.sin(2 * np.pi * turns / size)
    return {
        "x": x,
        "gate_w": np.concatenate([np.asarray(inputs[f"L0_conv_W{g}"]) for g in "fid"], 1),
        "gate_b": np.concatenate([np.asarray(inputs[f"L0_conv_b{g}"]) for g in "fid"]),
        "taps": taps,
        "dft": dft,
        "row_pick": np.eye(128, 3, dtype=np.float32),
        "ident": np.eye(128, dtype=np.float32),
        "ffn_w": np.ascontiguousarray(inputs["L0_ffn_W"]),
        "ffn_v": np.ascontiguousarray(inputs["L0_ffn_V"]),
        "gamma": np.asarray(inputs["L0_ffn_gamma"]).reshape(128, 1),
        "beta": np.asarray(inputs["L0_ffn_beta"]).reshape(128, 1),
    }


def kernel(**inputs):
    import numpy as _np
    import concourse.bacc as _bacc
    from concourse import mybir as _mybir
    from concourse.bass_utils import run_bass_kernel_spmd as _run

    nc = _bacc.Bacc("TRN2", target_bir_lowering=False, num_devices=1)
    arrays, args = {}, []
    for name, a in _layouts(inputs).items():
        a = _np.ascontiguousarray(a)
        arrays[f"in_{name}_dram"] = a
        args.append(nc.dram_tensor(f"in_{name}_dram", a.shape, _mybir.dt.from_np(a.dtype), kind="ExternalInput").ap())
    for i, (shape, dtype) in enumerate(_OUTS):
        dt = _mybir.dt.from_np(_np.dtype(dtype))
        args.append(nc.dram_tensor(f"out_{i}_dram", shape, dt, kind="ExternalOutput").ap())
    metaformer(nc, *args)
    r = _run(nc, [arrays], core_ids=[0])
    got = tuple(r.results[0][f"out_{i}_dram"] for i in range(len(_OUTS)))
    return got[0]
```

```python
from contextlib import ExitStack

import concourse.bass as bass
from concourse import mybir

F32 = mybir.dt.float32
BF16 = mybir.dt.bfloat16
I32 = mybir.dt.int32
ALU = mybir.AluOpType
ACT = mybir.ActivationFunctionType
AX = mybir.AxisListType

LN1_EPS = 1e-6
LN2_EPS = 1e-5
BN_EPS = 1e-5
SPECTRAL_EPS = 1e-8
SPECTRAL_RADIUS = 0.95

CHUNKS = 32
WARM_BLOCKS = 2
STEP_BLOCK = 8
START_TOL = 2.0 ** -19

ALL = "all"
CHAIN = [(name, part) for names, parts in (
    (["b_straight"], [ALL]), (["b_cross"], [ALL]),
    (["softplus"], [0, 1]), (["gain"], [0, 1]), (["trace1"], [ALL]), (["det1"], [ALL]),
    (["inp"], [0, 1]), (["a_straight", "a_cross"], [0]), (["inp"], [2, 3]), (["a_straight", "a_cross"], [1]),
    (["trace2"], [0, 1]), (["fah"], [0, 1]), (["trace4"], [0, 1]), (["n4"], [0, 1]), (["e1"], [ALL]), (["e2"], [0, 1]),
    (["b4"], [0, 1]), (["k2"], [0, 1]), (["dk2"], [0, 1]), (["fah"], [2, 3]), (["b4e2"], [ALL]), (["n2"], [ALL]),
    (["b2"], [0, 1]), (["k1"], [0, 1]), (["dk1"], [0, 1]), (["b2e1"], [0, 1]), (["b1"], [0, 1]),
    (["matrix_part", "scalar_part"], [0]), (["matrix_part", "scalar_part"], [1]),
) for name, part in ((n, p) for p in parts for n in names)]
SQUARES = ["trace1_sq", "det2", "trace1_half_sq", "trace2_sq", "det4", "trace2_half_sq", "trace4_half_sq", "scalar_coef"]


def metaformer(nc, x, gate_w, gate_b, taps, dft, row_pick, ident_in, ffn_w, ffn_v, gamma, beta, out):
    NB, ROWS, P, C = x.shape
    H = C // 2
    T = ROWS * P
    HB = NB // 2
    NGRP = NB // 4
    L = T // CHUNKS
    SB = STEP_BLOCK
    BLOCKS = L // SB
    COLS = CHUNKS * NB
    HALF = COLS // 2
    NTOK = NB * T
    TILES = CHUNKS
    assert NB * SB == P and C == P and ROWS % 2 == 0 and BLOCKS % 4 == 0 and BLOCKS >= 8 and TILES % 8 == 0

    def chain_at(r, name, part):
        step = next(step for step in ((name, part), (name, ALL), (name, 1)) if step in CHAIN)
        return r * len(CHAIN) + (CHAIN.index(step) + 1)

    def square_at(r, name, half):
        return r * (2 * len(SQUARES)) + (2 * SQUARES.index(name) + half + 1)

    x1_dram = nc.dram_tensor("x1_dram", [T, NB, C], F32, kind="Internal").ap()
    norm_dram = nc.dram_tensor("norm_dram", [2, T, NB], F32, kind="Internal").ap()

    with ExitStack() as whole:
        def sem(name):
            return whole.enter_context(nc.semaphore(name))

        def keep(name, shape, dt=F32):
            return whole.enter_context(nc.sbuf_tensor(name, shape, dt))

        ident = keep("ident", [P, P])
        gram = keep("gram", [P, C + 1])
        setup_loaded = sem("setup_loaded")
        gram_copied = sem("gram_copied")
        sync_step = sem("sync_step")

        with ExitStack() as ctx:
            def sb(name, shape, dt=F32):
                return ctx.enter_context(nc.sbuf_tensor(name, shape, dt))

            def pb(name, shape):
                return ctx.enter_context(nc.psum_tensor(name, shape, F32))

            X = [sb(f"x_row{i}", [P, NB, C]) for i in range(3)]
            XN = sb("xn", [P, NB, C])
            XNT = sb("xn_t", [P, NB, P])
            FGS = [sb(f"forget{i}", [P, NB, C]) for i in range(2)]
            IGS = [sb(f"in_gate{i}", [P, NB, C]) for i in range(2)]
            SP = sb("soft", [P, NB, C])
            RL = sb("soft_relu", [P, NB, C])
            PAS = [sb(f"prod_a{i}", [P, NB, C]) for i in range(2)]
            PBuf = sb("prod_b", [P, NB, C])
            VV = sb("inp_vec", [P, NB, C])
            LNX = sb("ln_x1", [P, NB, C + 2])
            FSUM, FPROD, TR1, DT1, HS1, DT2, TR2, TR4, HS2, DT4, HS4, NN = [
                sb(n, [P, NB, H]) for n in ("forget_sum", "forget_prod", "trace1", "det1", "half1", "det2", "trace2",
                                            "trace4", "half2", "det4", "half4", "n_coef")]
            KK, AC = DT4, TR4
            stats1 = sb("stats_x", [P, NB, 6])
            stats2 = sb("stats_x1", [P, NB, 6])
            eps1, eps2, inv_c = [sb(n, [P, NB]) for n in ("eps1", "eps2", "inv_c")]
            msum, mdif, vsum, minus_half_var, log_var, guess, newton, rstd1, nmr1, rstd2, nmr2 = [
                sb(n, [P, NB]) for n in ("msum", "mdif", "vsum", "minus_half_var", "log_var", "guess", "newton",
                                         "rstd_x", "nmr_x", "rstd_x1", "nmr_x1")]
            E = sb("dft_row", [P, P])
            taps_sb = sb("taps", [P, 5 * H])
            raw = sb("coef_raw", [P, 2 * H])
            msq = sb("mag_sq", [P, 2 * H])
            mag, mag2, minus_half_mag2, log_mag2, mag_guess, mag_newton, inv_mag, scale, sig = [
                sb(n, [P, H]) for n in ("mag", "mag2", "minus_half_mag2", "log_mag2", "mag_guess", "mag_newton", "inv_mag", "scale", "mag_sig")]
            mag_eps, radius, minus_one, minus_half, three_half, two = [
                sb(n, [P, H]) for n in ("mag_eps", "radius", "minus_one", "minus_half", "three_half", "two")]
            coef = [sb(f"coef{i}", [P, 7, H]) for i in range(2)]
            wg = sb("gate_w", [P, 3 * C])
            bias_all = sb("bias_all", [P, 3 * C])
            bias_rest = sb("bias_rest", [P, 3 * C])
            bias_part = sb("bias_part", [P, 3 * C], BF16)
            bias_rows = sb("bias_rows", [P, 3 * C], BF16)
            pick = sb("row_pick", [P, 3])
            ones_bf = sb("ones_bf", [P, P], BF16)

            psT = pb("ps_turn", [P, 4, P])
            psG = pb("ps_gate", [P, 4, 512])
            psA = [pb(f"ps_add{i}", [P, 4, P]) for i in range(2)]
            psM = pb("ps_gram", [P, 512])

            setup = sem("setup")
            x_loaded = sem("x_loaded")
            dft_loaded = sem("dft_loaded")
            x1_stored = sem("x1_stored")
            norm_stored = sem("norm_stored")
            stats1_ready = sem("stats1_ready")
            stats2_ready = sem("stats2_ready")
            norm1_step = sem("norm1_step")
            norm2_step = sem("norm2_step_x1")
            var1_ready = sem("var1_ready")
            var2_ready = sem("var2_ready")
            log1_done = sem("log1_done")
            log2_done = sem("log2_done")
            log_mag_done = sem("log_mag_done")
            guess1_ready = sem("guess1_ready")
            guess2_ready = sem("guess2_ready")
            norm1_ready = sem("norm1_ready")
            norm2_ready = sem("norm2_ready")
            forget_pairs = sem("forget_pairs")
            coef_step = sem("coef_step")
            xn_ready = sem("xn_ready")
            xn_turned = sem("xn_turned")
            xnt_ready = sem("xnt_ready")
            gate_sums = sem("gate_sums")
            gate_read = sem("gate_read")
            soft_exp = sem("soft_exp")
            soft_ready = sem("soft_ready")
            chain = sem("chain")
            squares = sem("squares")
            bx_sums = sem("bx_sums")
            ah_sums = sem("ah_sums")
            n_sums = sem("n_sums")
            x1_sums = sem("x1_sums")
            x1_copied = sem("x1_copied")
            lnx_ready = sem("lnx_ready")
            gram_added = sem("gram_added")
            coef_sums = sem("coef_sums")
            coef_raw = sem("coef_raw")
            mag2_ready = sem("mag2_ready")
            mag_guess_ready = sem("mag_guess_ready")
            mag_ready = sem("mag_ready")
            mag_sig = sem("mag_sig")
            coef_ready = sem("coef_ready")

            SETUP_STEPS = 9

            block = ctx.enter_context(nc.Block())

            def rows(eng, row):
                row(-1, 5)
                row(0, 0)
                row(1, 1)
                turns = (ROWS - 5) // 6
                with eng.Fori(0, turns) as i:
                    for m in range(2, 8):
                        row(6 * i + m, m % 6)
                for r in range(6 * turns + 2, ROWS + 1):
                    row(r, r % 6)

            def fixed(r):
                return isinstance(r, int)

            def from_row(r, first):
                return not fixed(r) or r >= first

            def has_next(r):
                return not fixed(r) or r + 1 < ROWS

            def has_chain(r):
                return not fixed(r) or 0 <= r < ROWS

            def has_last(r):
                return from_row(r, 1)

            def x_of(m, ahead):
                return X[(m + ahead) % 3]

            def four(buf, g):
                return buf[:, 4 * g:4 * g + 4, :]

            @block.sync
            def _(sp):
                for dst, src in ((ident[:, :], ident_in), (wg[:, :], gate_w), (taps_sb[:, :], taps),
                                 (pick[:, :], row_pick), (bias_all[:, :], gate_b.partition_broadcast(P))):
                    sp.dma_start(dst, src).then_inc(setup_loaded, 16)
                x_rows = x.rearrange("b r w c -> r w b c")
                x1_rows = x1_dram.rearrange("(r w) b c -> r w b c", w=P)
                norm_rows = norm_dram.rearrange("i (r w) b -> i r w b", w=P)

                def load(r, buf):
                    for b in (0, HB):
                        sp.dma_start(buf[:, b:b + HB, :],
                                     x_rows[bass.ds(r, 1), :, b:b + HB].rearrange("o w b c -> w (o b) c")).then_inc(x_loaded, 16)
                    sp.dma_start(E[:, :], dft[bass.ds(r, 1)].rearrange("o k w -> k (o w)")).then_inc(dft_loaded, 16)

                def row(r, m):
                    if fixed(r) and r < 0:
                        load(0, X[0])
                        sp.wait_ge(x_loaded, 32)
                        sp.wait_ge(coef_sums, 1)
                        load(1, X[1])
                        return
                    if has_last(r):
                        sp.wait_ge(x1_copied, NGRP * r)
                        sp.sem_inc(sync_step, 1)
                        sp.dma_start(x1_rows[bass.ds(r - 1, 1)].rearrange("o w b c -> w (o b) c"),
                                     x_of(m, -1)[:, :, :]).then_inc(x1_stored, 16)
                        sp.wait_ge(norm2_ready, r)
                        sp.sem_inc(sync_step, 1)
                        for i, src in enumerate((rstd2, nmr2)):
                            sp.dma_start(norm_rows[i, bass.ds(r - 1, 1)].rearrange("o w b -> w (o b)"), src[:, :]).then_inc(norm_stored, 16)
                    if not fixed(r) or r + 2 < ROWS:
                        sp.wait_ge(coef_sums, r + 2)
                        sp.sem_inc(sync_step, 1)
                        if has_last(r):
                            sp.wait_ge(lnx_ready, 2 * r)
                            sp.sem_inc(sync_step, 1)
                            sp.wait_ge(x1_stored, 16 * r)
                            sp.sem_inc(sync_step, 1)
                        load(r + 2, x_of(m, 2))

                rows(sp, row)
                sp.wait_ge(x1_stored, 16 * ROWS)
                sp.wait_ge(norm_stored, 32 * ROWS)

            @block.tensor
            def _(pe):
                pe.wait_ge(setup, SETUP_STEPS)
                pe.wait_ge(setup_loaded, 16 * 5)

                nc.tensor.matmul(psM[:, 0:C + 1], LNX[:, 0, 0:C], LNX[:, 0, 0:C + 1], start=True, stop=False)

                def add_up(bank, g, *terms):
                    for t in terms:
                        last = nc.tensor.matmul(psA[bank][:, :, :], ident[:, :], four(t, g), start=t is terms[0], stop=t is terms[-1])
                    return last

                def row(r, m):
                    PA = PAS[m % 2]
                    if has_next(r):
                        pe.wait_ge(dft_loaded, 16 * (r + 2))
                        if from_row(r, 0):
                            pe.wait_ge(xnt_ready, NGRP * (r + 1))
                        nc.tensor.matmul(psT[:, :, :].rearrange("p a b -> p (a b)")[:, 0:5 * H], E[:, :], taps_sb[:, :], start=True, stop=True).then_inc(coef_sums, 1)
                    if has_last(r):
                        for g in range(4):
                            if g < 2:
                                pe.wait_ge(squares, square_at(r - 1, "scalar_coef", g))
                            else:
                                pe.wait_ge(x1_copied, NGRP * (r - 1) + g - 1)
                            pe.wait_ge(chain, chain_at(r - 1, "scalar_part", g // 2))
                            add_up(g % 2, g, x_of(m, -1), PAS[(m + 1) % 2], VV).then_inc(x1_sums, 1)

                    def bx(g):
                        if g >= 2:
                            pe.wait_ge(chain, chain_at(r, "inp", g - 2))
                        elif has_last(r):
                            pe.wait_ge(x1_copied, NGRP * (r - 1) + g + 3)
                        pe.wait_ge(chain, chain_at(r, "b_cross", g // 2))
                        add_up(g % 2, g, PA, PBuf).then_inc(bx_sums, 1)

                    def ah(g):
                        pe.wait_ge(chain, chain_at(r, "inp", g + 2) if g < 2 else chain_at(r, "fah", g - 2))
                        pe.wait_ge(chain, chain_at(r, "a_cross", g // 2))
                        add_up(g % 2, g, PA, PBuf).then_inc(ah_sums, 1)

                    def n1():
                        for h in range(2):
                            pe.wait_ge(chain, chain_at(r, "dk1", h))
                            for t in (KK, NN):
                                last = nc.tensor.matmul(psA[h][:, :, :].rearrange("p a b -> p (a b)"), ident[:, :],
                                                        t[:, h * HB:(h + 1) * HB, :].rearrange("p b c -> p (b c)"), start=t is KK, stop=t is NN)
                            last.then_inc(n_sums, 1)

                    def add_gram(half):
                        pe.wait_ge(lnx_ready, 2 * (r - 1) + half + 1)
                        for b in range(half * HB, (half + 1) * HB):
                            last = nc.tensor.matmul(psM[:, 0:C + 1], LNX[:, b, 0:C], LNX[:, b, 0:C + 1], start=False,
                                                    stop=fixed(r) and r == ROWS and b == NB - 1)
                        last.then_inc(gram_added, 1)

                    def gates(g):
                        if not has_next(r):
                            return
                        pe.wait_ge(xnt_ready, NGRP * (r + 1) + g + 1)
                        if from_row(r, 0) or g >= 1:
                            pe.wait_ge(gate_read, NGRP * (r + 1) + g)
                        for b in range(4):
                            nc.tensor.matmul(psG[:, b, 0:3 * C], ones_bf[0:32, :], bias_rows[0:32, :], start=True, stop=False)
                            last = nc.tensor.matmul(psG[:, b, 0:3 * C], XNT[:, 4 * g + b, :], wg[:, :], start=False, stop=True)
                        last.then_inc(gate_sums, 1)

                    if has_chain(r):
                        bx(0)
                        bx(1)
                    if has_next(r):
                        for g in range(NGRP):
                            pe.wait_ge(xn_ready, NGRP * (r + 1) + g + 1)
                            if g == 0:
                                pe.wait_ge(coef_raw, r + 2)
                            else:
                                pe.wait_ge(xnt_ready, NGRP * (r + 1) + g)
                            for b in range(4):
                                last = nc.tensor.transpose(psT[:, b, :], XN[:, 4 * g + b, :], ident[:, :])
                            last.then_inc(xn_turned, 1)
                            if g < 2 and has_chain(r):
                                bx(g + 2)
                            if g == 2:
                                gates(0)
                    elif has_chain(r):
                        bx(2)
                        bx(3)
                    if has_chain(r):
                        ah(0)
                        ah(1)
                        ah(2)
                        ah(3)
                    gates(1)
                    if has_last(r):
                        add_gram(0)
                    gates(2)
                    if has_last(r):
                        add_gram(1)
                    if has_chain(r):
                        n1()
                    gates(3)

                rows(pe, row)

            @block.gpsimd
            def _(pool):
                NORM_STEPS, COEF_STEPS = 9, 15
                pool.wait_ge(setup, SETUP_STEPS)
                TT = nc.gpsimd.tensor_tensor

                def counted(count, base):
                    n = [0]

                    def then(ins):
                        n[0] += 1
                        ins.then_inc(count, 1)
                        pool.wait_ge(count, base + n[0])

                    return then

                def moments(then, stats, eps, var_ready, guess_ready, nth, rstd, nmr, free):
                    half = minus_half[:, 0:NB]
                    TT(msum[:, :], stats[:, :, 1], stats[:, :, 4], ALU.add)
                    TT(mdif[:, :], stats[:, :, 1], stats[:, :, 4], ALU.subtract)
                    then(TT(vsum[:, :], stats[:, :, 2], stats[:, :, 5], ALU.add))
                    then(TT(mdif[:, :], mdif[:, :], half, ALU.mult))
                    TT(vsum[:, :], vsum[:, :], inv_c[:, :], ALU.mult)
                    then(TT(mdif[:, :], mdif[:, :], mdif[:, :], ALU.mult))
                    then(TT(vsum[:, :], vsum[:, :], mdif[:, :], ALU.add))
                    TT(vsum[:, :], vsum[:, :], eps[:, :], ALU.add).then_inc(var_ready, 1)
                    pool.wait_ge(var_ready, nth)
                    TT(minus_half_var[:, :], vsum[:, :], half, ALU.mult)
                    then(TT(msum[:, :], msum[:, :], half, ALU.mult))
                    pool.wait_ge(guess_ready, nth)
                    then(TT(newton[:, :], guess[:, :], guess[:, :], ALU.mult))
                    then(TT(newton[:, :], newton[:, :], minus_half_var[:, :], ALU.mult))
                    then(TT(newton[:, :], newton[:, :], three_half[:, 0:NB], ALU.add))
                    free()
                    then(TT(rstd[:, :], newton[:, :], guess[:, :], ALU.mult))
                    return TT(nmr[:, :], msum[:, :], rstd[:, :], ALU.mult)

                def row(r, m):
                    q = coef[(m + 1) % 2]
                    coef_then = counted(coef_step, COEF_STEPS * (r + 1))

                    def pairs(dst, op):
                        FG = FGS[m % 2]
                        return TT(dst[:, :, :], FG[:, :, 0:H], FG[:, :, H:C], op)

                    if has_chain(r):
                        pool.wait_ge(gate_read, NGRP * (r + 1))
                        if from_row(r, 1):
                            pool.wait_ge(chain, chain_at(r - 1, "det1", 1))
                        pairs(FPROD, ALU.mult)
                    if has_chain(r):
                        pool.wait_ge(chain, chain_at(r, "b_cross", 1))
                        pairs(FSUM, ALU.add).then_inc(forget_pairs, 1)
                    if has_next(r):
                        def free1():
                            if from_row(r, 0):
                                pool.wait_ge(xn_ready, NGRP * (r + 1))

                        pool.wait_ge(stats1_ready, r + 2)
                        moments(counted(norm1_step, NORM_STEPS * (r + 1)), stats1, eps1, var1_ready, guess1_ready, r + 2,
                                rstd1, nmr1, free1).then_inc(norm1_ready, 1)
                        pool.wait_ge(coef_raw, r + 2)
                        coef_then(TT(msq[:, :], raw[:, :], raw[:, :], ALU.mult))
                        coef_then(TT(mag2[:, :], msq[:, 0:H], msq[:, H:2 * H], ALU.add))
                        TT(mag2[:, :], mag2[:, :], mag_eps[:, :], ALU.add).then_inc(mag2_ready, 1)
                        pool.wait_ge(mag2_ready, r + 2)
                        coef_then(TT(minus_half_mag2[:, :], mag2[:, :], minus_half[:, :], ALU.mult))
                        pool.wait_ge(mag_guess_ready, r + 2)
                        coef_then(TT(mag_newton[:, :], mag_guess[:, :], mag_guess[:, :], ALU.mult))
                        coef_then(TT(mag_newton[:, :], mag_newton[:, :], minus_half_mag2[:, :], ALU.mult))
                        coef_then(TT(mag_newton[:, :], mag_newton[:, :], three_half[:, :], ALU.add))
                        coef_then(TT(inv_mag[:, :], mag_newton[:, :], mag_guess[:, :], ALU.mult))
                        TT(mag[:, :], mag2[:, :], inv_mag[:, :], ALU.mult).then_inc(mag_ready, 1)
                        pool.wait_ge(mag_ready, r + 2)
                        coef_then(TT(mag2[:, :], mag[:, :], mag_eps[:, :], ALU.add))
                        coef_then(TT(mag2[:, :], mag2[:, :], inv_mag[:, :], ALU.mult))
                        coef_then(TT(mag2[:, :], two[:, :], mag2[:, :], ALU.subtract))
                        coef_then(TT(mag2[:, :], mag2[:, :], inv_mag[:, :], ALU.mult))
                        coef_then(TT(scale[:, :], mag2[:, :], radius[:, :], ALU.mult))
                    if has_last(r):
                        def free2():
                            if from_row(r, 2):
                                pool.wait_ge(lnx_ready, 2 * (r - 1))
                                pool.wait_ge(norm_stored, 32 * (r - 1))

                        if has_next(r):
                            pool.wait_ge(norm1_ready, r + 2)
                        pool.wait_ge(stats2_ready, r)
                        moments(counted(norm2_step, NORM_STEPS * (r - 1)), stats2, eps2, var2_ready, guess2_ready, r,
                                rstd2, nmr2, free2).then_inc(norm2_ready, 1)
                    if has_next(r):
                        pool.wait_ge(mag_sig, r + 2)
                        coef_then(TT(scale[:, :], scale[:, :], sig[:, :], ALU.mult))
                        TT(q[:, 0, :], raw[:, 0:H], scale[:, :], ALU.mult)
                        coef_then(TT(q[:, 2, :], raw[:, H:2 * H], scale[:, :], ALU.mult))
                        TT(q[:, 1, :], q[:, 2, :], minus_one[:, :], ALU.mult)
                        TT(msq[:, 0:H], q[:, 0, :], q[:, 0, :], ALU.mult)
                        coef_then(TT(msq[:, H:2 * H], q[:, 2, :], q[:, 2, :], ALU.mult))
                        TT(q[:, 3, :], msq[:, 0:H], msq[:, H:2 * H], ALU.add).then_inc(coef_ready, 1)

                rows(pool, row)

            @block.scalar
            def _(act):
                act.wait_ge(setup, SETUP_STEPS)
                act.preload_act_table_set("natural_log_exp_and_others")

                def halves(buf, h):
                    return buf[:, h * HB:(h + 1) * HB, :]

                def row(r, m):
                    def square(name, dst, src, after, bias=0.0):
                        for h in range(2):
                            act.wait_ge(chain, chain_at(r, after, h))
                            nc.scalar.activation(halves(dst, h), halves(src, h), ACT.Square, bias=bias).then_inc(squares, 1)

                    def gates(g):
                        if not has_next(r):
                            return
                        act.wait_ge(gate_sums, NGRP * (r + 1) + g + 1)
                        if g == 0 and has_last(r):
                            act.wait_ge(forget_pairs, r)
                        nc.scalar.activation(four(FGS[(m + 1) % 2], g), psG[:, :, 0:C], ACT.Sigmoid)
                        nc.scalar.activation(four(IGS[(m + 1) % 2], g), psG[:, :, C:2 * C], ACT.Sigmoid)
                        nc.scalar.activation(four(RL, g), psG[:, :, 2 * C:3 * C], ACT.Relu)
                        nc.scalar.activation(four(SP, g), psG[:, :, 2 * C:3 * C], ACT.Abs).then_inc(gate_read, 1)

                    def inverse_root(src, log, dst, ready, nth, log_done, done):
                        act.wait_ge(ready, nth)
                        nc.scalar.activation(log[:, :], src[:, :], ACT.Ln).then_inc(log_done, 1)
                        act.wait_ge(log_done, nth)
                        nc.scalar.activation(dst[:, :], log[:, :], ACT.Exp, scale=-0.5).then_inc(done, 1)

                    def mag_root():
                        if has_next(r):
                            inverse_root(mag2, log_mag2, mag_guess, mag2_ready, r + 2, log_mag_done, mag_guess_ready)

                    def between():
                        if has_chain(r):
                            for h in range(2):
                                act.wait_ge(soft_exp, 2 * r + h + 1)
                                nc.scalar.activation(halves(SP, h), halves(SP, h), ACT.Ln, bias=1.0).then_inc(soft_ready, 1)
                        if not has_next(r):
                            return
                        act.wait_ge(coef_sums, r + 2)
                        if from_row(r, 0):
                            act.wait_ge(coef_ready, r + 1)
                        if from_row(r, 1):
                            act.wait_ge(chain, chain_at(r - 1, "a_cross", 1))
                        sums = psT[:, :, :].rearrange("p a b -> p (a b)")
                        nc.scalar.activation(coef[(m + 1) % 2][:, 4:7, :].rearrange("p k c -> p (k c)"), sums[:, 2 * H:5 * H], ACT.Identity)
                        nc.scalar.activation(raw[:, :], sums[:, 0:2 * H], ACT.Identity).then_inc(coef_raw, 1)

                    def xn(g):
                        for b in range(4 * g, 4 * g + 4):
                            last = nc.scalar.activation(XN[:, b, :], x_of(m, 1)[:, b, :], ACT.Identity,
                                                        bias=nmr1[:, b:b + 1], scale=rstd1[:, b:b + 1])
                        last.then_inc(xn_ready, 1)

                    def lnx(first):
                        for b in range(first, first + HB):
                            last = nc.scalar.activation(LNX[:, b, 0:C], x_of(m, -1)[:, b, :], ACT.Identity,
                                                        bias=nmr2[:, b:b + 1], scale=rstd2[:, b:b + 1])
                        last.then_inc(lnx_ready, 1)

                    def xnt(g):
                        act.wait_ge(xn_turned, NGRP * (r + 1) + g + 1)
                        nc.scalar.activation(four(XNT, g), psT[:, :, :], ACT.Identity).then_inc(xnt_ready, 1)

                    if has_last(r):
                        for g in range(NGRP):
                            if g == 2:
                                between()
                            act.wait_ge(x1_sums, NGRP * (r - 1) + g + 1)
                            nc.scalar.activation(four(x_of(m, -1), g), psA[g % 2][:, :, :], ACT.Identity).then_inc(x1_copied, 1)
                    else:
                        between()
                    if has_next(r):
                        inverse_root(vsum, log_var, guess, var1_ready, r + 2, log1_done, guess1_ready)
                        act.wait_ge(norm1_ready, r + 2)
                        if from_row(r, 0):
                            act.wait_ge(chain, chain_at(r, "b_cross", 1))
                        xn(0)
                        xn(1)
                        mag_root()
                        xnt(0)
                        xn(2)
                        xnt(1)
                    if has_chain(r):
                        square("trace1_sq", TR2, TR1, "trace1")
                        square("det2", DT2, DT1, "det1")
                    if has_next(r):
                        xn(3)
                        xnt(2)
                        xnt(3)
                    if has_chain(r):
                        square("trace1_half_sq", HS1, TR1, "trace1", 0.5)
                    if has_last(r):
                        inverse_root(vsum, log_var, guess, var2_ready, r, log2_done, guess2_ready)
                    if has_chain(r):
                        square("trace2_sq", TR4, TR2, "trace2")
                        square("det4", DT4, DT2, "trace2")
                    gates(0)
                    if has_chain(r):
                        square("trace2_half_sq", HS2, TR2, "trace2", 0.5)
                        square("trace4_half_sq", HS4, TR4, "trace4", 0.5)
                    if has_next(r):
                        act.wait_ge(mag_ready, r + 2)
                        nc.scalar.activation(sig[:, :], mag[:, :], ACT.Sigmoid).then_inc(mag_sig, 1)
                    if has_last(r):
                        act.wait_ge(norm2_ready, r)
                        if from_row(r, 2):
                            act.wait_ge(gram_added, 2 * (r - 1))
                        lnx(0)
                    gates(1)
                    if has_last(r):
                        lnx(HB)
                    gates(2)
                    if has_chain(r):
                        for h in range(2):
                            act.wait_ge(n_sums, 2 * r + h + 1)
                            nc.scalar.activation(halves(AC, h).rearrange("p b c -> p (b c)"), psA[h][:, :, :].rearrange("p a b -> p (a b)"),
                                                 ACT.Identity, scale=-1.0, bias=1.0).then_inc(squares, 1)
                    gates(3)
                    if has_next(r):
                        act.preload_act_table_set("natural_log_exp_and_others")
                        act.wait_ge(gate_read, NGRP * (r + 2))
                        for h in range(2):
                            nc.scalar.activation(halves(SP, h), halves(SP, h), ACT.Exp, scale=-1.0).then_inc(soft_exp, 1)

                rows(act, row)

            @block.vector
            def _(v):
                done = [0]

                def step(ins):
                    done[0] += 1
                    ins.then_inc(setup, 1)
                    v.wait_ge(setup, done[0])

                V = nc.vector
                V.memset(eps1[:, :], LN1_EPS)
                V.memset(eps2[:, :], LN2_EPS)
                V.memset(minus_half[:, :], -0.5)
                V.memset(three_half[:, :], 1.5)
                V.memset(two[:, :], 2.0)
                V.memset(inv_c[:, :], 1.0 / C)
                V.memset(mag_eps[:, :], SPECTRAL_EPS)
                V.memset(radius[:, :], SPECTRAL_RADIUS)
                V.memset(minus_one[:, :], -1.0)
                V.memset(ones_bf[:, :], 1.0)
                step(V.memset(LNX[:, :, :], 0.0))
                v.wait_ge(setup_loaded, 16 * 5)
                V.tensor_scalar(taps_sb[64:P, H:2 * H], taps_sb[64:P, H:2 * H], -1.0, None, ALU.mult)
                V.tensor_scalar(taps_sb[0:64, 3 * H:4 * H], taps_sb[0:64, 3 * H:4 * H], -1.0, None, ALU.mult)
                V.tensor_scalar(taps_sb[64:P, 4 * H:5 * H], taps_sb[64:P, 4 * H:5 * H], -1.0, None, ALU.mult)
                V.memset(LNX[:, :, C:C + 1], 1.0)
                step(V.tensor_scalar(bias_all[:, 0:C], bias_all[:, 0:C], 2.0, None, ALU.add))
                step(V.tensor_copy(bias_part[:, :], bias_all[:, :]))
                V.tensor_tensor(bias_rest[:, :], bias_all[:, :], bias_part[:, :], ALU.subtract)
                step(V.tensor_scalar(bias_rows[:, :], bias_part[:, :], pick[:, 0:1], None, ALU.mult))
                step(V.tensor_copy(bias_part[:, :], bias_rest[:, :]))
                step(V.tensor_tensor(bias_rest[:, :], bias_rest[:, :], bias_part[:, :], ALU.subtract))
                step(V.scalar_tensor_tensor(bias_rows[:, :], bias_part[:, :], pick[:, 1:2], bias_rows[:, :], ALU.mult, ALU.add))
                step(V.tensor_copy(bias_part[:, :], bias_rest[:, :]))
                step(V.scalar_tensor_tensor(bias_rows[:, :], bias_part[:, :], pick[:, 2:3], bias_rows[:, :], ALU.mult, ALU.add))

                def batches(h):
                    return slice(0, NB) if h is ALL else slice(h * HB, (h + 1) * HB)

                def full(buf, h):
                    return buf[:, batches(h), :].rearrange("p b (k c) -> p b k c", k=2)

                def crossed(buf, h):
                    return full(buf, h)[:, :, ::-1, :]

                def pair(buf, h):
                    return buf[:, batches(h), :]

                def both(buf, h):
                    return pair(buf, h).unsqueeze(2).broadcast_to([P, HB, 2, H])

                STT, TT = V.scalar_tensor_tensor, V.tensor_tensor
                M, A, S = ALU.mult, ALU.add, ALU.subtract

                def row(r, m):
                    q, FG, IG, PA = coef[m % 2], FGS[m % 2], IGS[m % 2], PAS[m % 2]
                    order = iter(CHAIN)

                    def cf(k):
                        return q[:, k, :].unsqueeze(1).broadcast_to([P, NB, H])

                    def cf2(k, same, n=HB):
                        a = q[:, k:k + 1, :].broadcast_to([P, 2, H]) if same else q[:, k:k + 2, :]
                        return a.unsqueeze(1).broadcast_to([P, n, 2, H])

                    def at(name, make, parts=(0, 1), needs=None, square=None, sums=None):
                        for p in parts if (name, 0) in CHAIN else (ALL,):
                            assert next(order) == (name, p)
                            if needs:
                                v.wait_ge(chain, chain_at(r, needs, p // 2 if sums else p))
                            if square:
                                v.wait_ge(squares, square_at(r, square, 1 if p is ALL else p))
                            if sums:
                                v.wait_ge(sums, NGRP * r + p + 1)
                            make(p).then_inc(chain, 1)

                    if has_chain(r):
                        v.wait_ge(coef_ready, r + 1)
                        v.wait_ge(xn_ready, NGRP * (r + 1))
                        at("b_straight", lambda h: TT(full(PA, h), full(XN, h), cf2(4, True, NB), M))
                        at("b_cross", lambda h: TT(full(PBuf, h), crossed(XN, h), cf2(5, False, NB), M))
                    if has_next(r):
                        v.wait_ge(x_loaded, 32 * (r + 2))
                        if from_row(r, 0):
                            v.wait_ge(norm1_ready, r + 1)
                        for b in range(NB):
                            last = V.bn_stats(stats1[:, b, :], x_of(m, 1)[:, b, :])
                        last.then_inc(stats1_ready, 1)
                    if has_chain(r):
                        v.wait_ge(soft_ready, 2 * r + 2)
                        at("softplus", lambda h: TT(full(SP, h), full(SP, h), full(RL, h), A))
                        at("gain", lambda h: STT(full(IG, h), full(SP, h), 0.1, full(IG, h), M, M), needs="softplus")
                        v.wait_ge(forget_pairs, r + 1)
                        at("trace1", lambda h: TT(pair(TR1, h), pair(FSUM, h), cf(0), M))
                        at("det1", lambda h: TT(pair(DT1, h), pair(FPROD, h), cf(3), M))
                    inp = lambda g: TT(four(VV, g), psA[g % 2][:, :, :], four(IG, g), M)
                    fah = lambda g: TT(four(PA, g), psA[g % 2][:, :, :], four(FG, g), M)
                    a_straight = lambda h: TT(full(PA, h), full(VV, h), cf2(0, True), M)
                    a_cross = lambda h: TT(full(PBuf, h), crossed(VV, h), cf2(1, False), M)
                    if has_chain(r):
                        at("inp", inp, [0, 1], needs="gain", sums=bx_sums)
                        v.wait_ge(chain, chain_at(r, "inp", 1))
                        at("a_straight", a_straight, [0])
                        at("a_cross", a_cross, [0])
                    if has_last(r):
                        v.wait_ge(x1_copied, NGRP * r)
                        if from_row(r, 2):
                            v.wait_ge(norm2_ready, r - 1)
                        for b in range(NB):
                            last = V.bn_stats(stats2[:, b, :], x_of(m, -1)[:, b, :])
                        last.then_inc(stats2_ready, 1)
                    if not has_chain(r):
                        return
                    at("inp", inp, [2, 3], needs="gain", sums=bx_sums)
                    v.wait_ge(chain, chain_at(r, "inp", 3))
                    at("a_straight", a_straight, [1])
                    at("a_cross", a_cross, [1])
                    at("trace2", lambda h: STT(pair(TR2, h), pair(DT1, h), -2.0, pair(TR2, h), M, A), square="det2")
                    at("fah", fah, [0, 1], sums=ah_sums)
                    at("trace4", lambda h: STT(pair(TR4, h), pair(DT2, h), -2.0, pair(TR4, h), M, A), square="trace2_sq")
                    at("n4", lambda h: STT(pair(NN, h), pair(TR4, h), 1.0, pair(DT4, h), A, M), needs="trace4", square="det4")
                    at("e1", lambda h: STT(pair(HS1, h), pair(HS1, h), -0.25, pair(DT1, h), A, S), square="trace1_half_sq")
                    at("e2", lambda h: STT(pair(HS2, h), pair(HS2, h), -0.25, pair(DT2, h), A, S), square="trace2_half_sq")
                    at("b4", lambda h: STT(pair(HS4, h), pair(HS4, h), 0.75, pair(DT4, h), A, S), square="trace4_half_sq")
                    at("k2", lambda h: STT(pair(KK, h), pair(TR2, h), 1.0, pair(HS4, h), A, M), needs="b4")
                    at("dk2", lambda h: TT(pair(KK, h), pair(KK, h), pair(DT2, h), M), needs="k2")
                    at("fah", fah, [2, 3], sums=ah_sums)
                    at("b4e2", lambda h: TT(pair(HS4, h), pair(HS4, h), pair(HS2, h), M), needs="e2")
                    at("n2", lambda h: TT(pair(KK, h), pair(KK, h), pair(NN, h), A), needs="dk2")
                    at("b2", lambda h: STT(pair(HS2, h), pair(HS4, h), 1.0, pair(NN, h), A, S), needs="b4e2")
                    at("k1", lambda h: STT(pair(NN, h), pair(TR1, h), 1.0, pair(HS2, h), A, M), needs="b2")
                    at("dk1", lambda h: TT(pair(NN, h), pair(NN, h), pair(DT1, h), M), needs="k1")
                    at("b2e1", lambda h: TT(pair(HS2, h), pair(HS2, h), pair(HS1, h), M))
                    at("b1", lambda h: STT(pair(HS2, h), pair(HS2, h), 1.0, pair(KK, h), A, S), needs="b2e1")
                    for h in range(2):
                        at("matrix_part", lambda h: TT(full(PA, h), full(PA, h), both(HS2, h), M), [h], needs="b1")
                        at("scalar_part", lambda h: TT(full(VV, h), full(VV, h), both(AC, h), M), [h], square="scalar_coef")

                rows(v, row)
                v.wait_ge(gram_added, 2 * ROWS)
                V.tensor_copy(gram[:, :], psM[:, 0:C + 1]).then_inc(gram_copied, 1)

        with ExitStack() as ctx:
            def sb(name, shape, dt=F32):
                return ctx.enter_context(nc.sbuf_tensor(name, shape, dt))

            def pb(name, shape):
                return ctx.enter_context(nc.psum_tensor(name, shape, F32))

            XT = [sb(f"x1_block{i}", [P, TILES, C]) for i in range(4)]
            OUT = [sb(f"out_half{i}", [P, TILES // 2, C]) for i in range(2)]
            LN = [sb(f"ln_block{i}", [P, TILES, C]) for i in range(2)]
            LNT = [sb(f"ln_t{i}", [P, CHUNKS, SB, NB]) for i in range(2)]
            Y = [sb(f"y_t{i}", [P, CHUNKS, SB, NB]) for i in range(2)]
            START = sb("start", [P, CHUNKS, NB])
            NEXT = sb("next_start", [P, CHUNKS, NB])
            NORMS = [sb(f"norm_block{i}", [P, P]) for i in range(4)]
            NORM = [sb(f"norm{i}", [P, 2 * TILES]) for i in range(2)]
            minus_half = sb("minus_half2", [P, 1])
            w_sb, v_sb, w_t, v_t, prod, ws_t = [sb(n, [P, C]) for n in ("w_sb", "v_sb", "w_t", "v_t", "prod", "ws_t")]
            vec = sb("vec", [P, 16])
            ones = sb("ones", [P, 1])
            worst = sb("worst", [P, 2])
            flag = sb("flag", [1, 2], I32)

            psZ = [[pb(f"ps_z{g}{i}", [P, 512]) for i in range(2)] for g in range(2)]
            psI = [pb(f"ps_in{i}", [P, 4, P]) for i in range(2)]
            psO = [pb(f"ps_out{i}", [P, 4, P]) for i in range(2)]
            LOAD_CHUNKS = min(8, CHUNKS // 2)
            LOADED = 16 * (CHUNKS // 2 // LOAD_CHUNKS)
            GROUPS = TILES // 4

            loaded2 = sem("loaded2")
            fold = sem("fold")
            fold_pe = sem("fold_pe")
            fold_pool = sem("fold_pool")
            x_block = [sem(f"x_block{h}") for h in range(2)]
            norm_block = sem("norm_block")
            norm_turned = sem("norm_turned")
            norm_copied = sem("norm_copied")
            ln_block = sem("ln_block")
            ln_turned = sem("ln_turned")
            lnt_copied = sem("lnt_copied")
            z_ready = [sem(f"z_ready{g}") for g in range(2)]
            y_ready = [sem(f"y_ready{g}") for g in range(2)]
            y_turned = sem("y_turned")
            added = sem("added")
            out_stored = [sem(f"out_stored{h}") for h in range(2)]
            start_set = sem("start_set")
            check_step = sem("check_step")
            worst_max = sem("worst_max")
            worst_turned = sem("worst_turned")
            flag_set = sem("flag_set")
            verdict_seen = sem("verdict_seen")

            blocks_v = x1_dram.rearrange("(j n t) b c -> n (t b) j c", n=BLOCKS, t=SB)
            norms_v = norm_dram.rearrange("i (j n t) b -> i n j (t b)", n=BLOCKS, t=SB)
            out_v = out.rearrange("b r w c -> b (r w) c").rearrange("b (j n t) c -> n t b j c", n=BLOCKS, t=SB)
            FOLD_TURNED, FOLD_PROD, FOLD_VAR, FOLD_SCALED, FOLD_STEPS = 3, 4, 8, 12, 13
            SWEEPS = CHUNKS
            INNER = 4

            block = ctx.enter_context(nc.Block())

            def q_of(k, n):
                return n if k is None else WARM_BLOCKS + k * BLOCKS + n

            def n_blocks(k):
                return WARM_BLOCKS if k is None else BLOCKS

            def run_blocks(eng, k, body):
                if k is None:
                    for n in range(WARM_BLOCKS):
                        body(n, n % 4)
                    return
                for n in range(4):
                    body(n, (n + WARM_BLOCKS) % 4)
                if BLOCKS > 8:
                    with eng.Fori(1, BLOCKS // 4 - 1) as i:
                        for m in range(4):
                            body(4 * i + m, (m + WARM_BLOCKS) % 4)
                for n in range(BLOCKS - 4, BLOCKS):
                    body(n, (n + WARM_BLOCKS) % 4)

            def sweeps(eng, sweep):
                sweep(None)
                eng.wait_ge(flag_set, 1)
                with eng.Fori(0, SWEEPS // INNER) as outer:
                    more = eng.value_load(flag[0:1, 0:1], min_val=0, max_val=1)
                    with eng.If(more == 1):
                        with eng.Fori(0, INNER) as inner:
                            again = eng.value_load(flag[0:1, 0:1], min_val=0, max_val=1)
                            with eng.If(again == 1):
                                k = outer * INNER + inner
                                sweep(k)
                                eng.wait_ge(flag_set, k + 2)
                                eng.sem_inc(verdict_seen, 1)

            def fixed(n):
                return isinstance(n, int)

            def chunks(g):
                return slice(g * CHUNKS // 2, (g + 1) * CHUNKS // 2)

            @block.sync
            def _(sp):
                sp.dma_start(w_sb[:, :], ffn_w).then_inc(loaded2, 16)
                sp.dma_start(v_sb[:, :], ffn_v).then_inc(loaded2, 16)
                sp.dma_start(vec[:, 0:1], gamma).then_inc(loaded2, 16)
                sp.dma_start(vec[:, 1:2], beta).then_inc(loaded2, 16)

                def sweep(k):
                    def source(n):
                        return n + (BLOCKS - WARM_BLOCKS) if k is None else n

                    def load_norms(n, slot):
                        if not (k is None and n == 0):
                            sp.wait_ge(norm_block, 32 * q_of(k, n))
                            sp.sem_inc(sync_step, 1)
                        for i in range(2):
                            sp.dma_start(NORMS[slot % 4][i * TILES:(i + 1) * TILES, :],
                                         norms_v[i, bass.ds(source(n), 1)].rearrange("o j p -> j (o p)")).then_inc(norm_block, 16)

                    def load(n, slot, h):
                        if not (k is None and n == 0):
                            sp.wait_ge(x_block[h], LOADED * q_of(k, n))
                            sp.sem_inc(sync_step, 1)
                        for j in range(h * CHUNKS // 2, (h + 1) * CHUNKS // 2, LOAD_CHUNKS):
                            sp.dma_start(XT[slot % 4][:, j:j + LOAD_CHUNKS, :],
                                         blocks_v[bass.ds(source(n), 1), :, j:j + LOAD_CHUNKS].rearrange("o p j c -> p (o j) c")).then_inc(x_block[h], 16)

                    if k is None:
                        for n in range(WARM_BLOCKS):
                            load_norms(n, n)
                            for h in range(2):
                                load(n, n, h)
                        return
                    sp.wait_ge(ln_block, q_of(k, 0))
                    sp.sem_inc(sync_step, 1)
                    for n in range(4):
                        load_norms(n, n + WARM_BLOCKS)
                        for h in range(2):
                            load(n, n + WARM_BLOCKS, h)

                    def store(n, slot):
                        more = not (fixed(n) and n + 4 >= BLOCKS)
                        if more:
                            sp.wait_ge(norm_turned, q_of(k, n) + 1)
                            sp.sem_inc(sync_step, 1)
                            load_norms(n + 4, slot)
                        for h in range(2):
                            sp.wait_ge(added, GROUPS * (k * BLOCKS + n) + GROUPS // 2 * (h + 1))
                            sp.sem_inc(sync_step, 1)
                            js = slice(h * TILES // 2, (h + 1) * TILES // 2)
                            for t in range(SB):
                                sp.dma_start(out_v[bass.ds(n, 1), t, :, js, :].rearrange("o b j c -> (o b) j c"),
                                             OUT[h][t * NB:(t + 1) * NB, :, :]).then_inc(out_stored[h], 16)
                            if more:
                                load(n + 4, slot, h)

                    run_blocks(sp, k, store)
                    for h in range(2):
                        sp.wait_ge(out_stored[h], 16 * SB * BLOCKS * (k + 1))
                        sp.sem_inc(sync_step, 1)

                sp.wait_ge(gram_copied, 1)
                sp.wait_ge(start_set, 1)
                sweeps(sp, sweep)

            @block.gpsimd
            def _(pool):
                pool.wait_ge(fold, FOLD_VAR)
                nc.gpsimd.tensor_tensor(vec[:, 6:7], vec[:, 5:6], minus_half[:, 0:1], ALU.pow).then_inc(fold_pool, 1)

            def per_step(total, first, last):
                steps = last - first
                return [total * (t + 1 - first) // steps - total * (t - first) // steps if first <= t < last else 0 for t in range(SB)]

            NORM_AT = 1
            IN_AT = per_step(GROUPS, 1, SB - 1)
            OUT_AT = per_step(GROUPS, 0, SB - 1)

            def zcount(k, n, t):
                return SB * q_of(k, n) + t

            @block.tensor
            def _(pe):
                pe.wait_ge(loaded2, 64)
                pe.wait_ge(gram_copied, 1)
                nc.tensor.transpose(psI[0][:, 0, :], w_sb[:, :], ident[:, :]).then_inc(fold_pe, 1)
                nc.tensor.transpose(psI[1][:, 1, :], v_sb[:, :], ident[:, :]).then_inc(fold_pe, 1)
                pe.wait_ge(fold, FOLD_TURNED)
                nc.tensor.matmul(psO[0][:, 0, 0:C], gram[:, 0:C], w_t[:, :], start=True, stop=True).then_inc(fold_pe, 1)
                nc.tensor.matmul(psO[1][:, 0, 0:1], w_t[:, :], gram[:, C:C + 1], start=True, stop=True).then_inc(fold_pe, 1)
                pe.wait_ge(fold, FOLD_PROD)
                nc.tensor.matmul(psI[1][:, 0, 0:1], prod[:, :], ones[:, :], start=True, stop=True).then_inc(fold_pe, 1)
                pe.wait_ge(fold, FOLD_SCALED)
                nc.tensor.transpose(psI[0][:, 0, :], prod[:, :], ident[:, :]).then_inc(fold_pe, 1)
                pe.wait_ge(fold, FOLD_STEPS)

                def turn_norms(k, n, slot):
                    q = q_of(k, n)
                    pe.wait_ge(norm_block, 32 * (q + 1))
                    if not (k is None and n == 0):
                        pe.wait_ge(norm_copied, q)
                    if not (k is None and n < 2):
                        pe.wait_ge(lnt_copied, GROUPS * (q - 1))
                    nc.tensor.transpose(psI[1][:, 0, :], NORMS[slot % 4][:, :], ident[:, :]).then_inc(norm_turned, 1)

                def turn_in(k, n, slot, g):
                    at = GROUPS * q_of(k, n) + g
                    if g == 0:
                        pe.wait_ge(ln_block, q_of(k, n) + 1)
                    if not (k is None and n == 0 and g < 2):
                        pe.wait_ge(lnt_copied, at - 1)
                    if g == 1:
                        ahead = q_of(k, n) + (1 if fixed(n) and n + 1 >= n_blocks(k) else 2)
                        pe.wait_ge(norm_copied, ahead)
                    for j in range(4):
                        last = nc.tensor.transpose(psI[g % 2][:, j, :], LN[slot % 2][:, 4 * g + j, :], ident[:, :])
                    last.then_inc(ln_turned, 1)

                def turn_out(k, n, slot, g):
                    at = GROUPS * (k * BLOCKS + n) + g
                    if not (fixed(n) and n == 0 and g < 2):
                        pe.wait_ge(added, at - 1)
                    for j in range(4):
                        last = nc.tensor.transpose(psO[g % 2][:, j, :], Y[slot % 2][:, 4 * g + j].rearrange("p t b -> p (t b)"), ident[:, :])
                    last.then_inc(y_turned, 1)

                def input_part(n_slot, g, t, stop=False):
                    nc.tensor.matmul(psZ[g][t % 2][:, 0:HALF], ws_t[:, :], LNT[n_slot % 2][:, chunks(g), t, :], start=True, stop=False)

                def sweep(k):
                    if k is None:
                        pe.wait_ge(start_set, 1)
                    slot0 = 0 if k is None else WARM_BLOCKS % 4
                    for n in range(2):
                        turn_norms(k, n, slot0 + n)
                    for g in range(GROUPS):
                        turn_in(k, 0, slot0, g)
                    pe.wait_ge(lnt_copied, GROUPS * (q_of(k, 0) + 1))
                    for g in range(2):
                        input_part(slot0, g, 0)

                    def steps(n, slot):
                        is_last = fixed(n) and n == n_blocks(k) - 1
                        is_first = fixed(n) and n == 0
                        gi = go = 0
                        for t in range(SB):
                            for g in range(2):
                                if t == 0 and is_first:
                                    rhs = START[:, chunks(g), :]
                                    if k is not None:
                                        pe.wait_ge(start_set, k + 2)
                                else:
                                    pe.wait_ge(y_ready[g], zcount(k, n, t))
                                    src = Y[slot % 2] if t else Y[(slot + 1) % 2]
                                    rhs = src[:, chunks(g), (t - 1) % SB, :]
                                nc.tensor.matmul(psZ[g][t % 2][:, 0:HALF], v_t[:, :], rhs, start=False, stop=True).then_inc(z_ready[g], 1)
                                if t + 1 < SB:
                                    input_part(slot, g, t + 1)
                                elif not is_last:
                                    if g == 0:
                                        pe.wait_ge(lnt_copied, GROUPS * (q_of(k, n) + 2))
                                    input_part(slot + 1, g, 0)
                                if t == NORM_AT and g == 0 and not (fixed(n) and n + 2 >= n_blocks(k)):
                                    turn_norms(k, n + 2, slot + 2)
                                if g == 0 and not is_last:
                                    for _ in range(IN_AT[t]):
                                        turn_in(k, n + 1, slot + 1, gi)
                                        gi += 1
                                if g == 1 and not is_first and k is not None:
                                    for _ in range(OUT_AT[t]):
                                        turn_out(k, n - 1, slot + 3, go)
                                        go += 1
                        if is_last and k is not None:
                            pe.wait_ge(y_ready[0], zcount(k, n, SB))
                            pe.wait_ge(y_ready[1], zcount(k, n, SB))
                            for g in range(GROUPS):
                                turn_out(k, n, slot, g)

                    run_blocks(pe, k, steps)
                    if k is not None:
                        pe.wait_ge(check_step, 2 * (k + 1))
                        nc.tensor.transpose(psI[0][0:1, 0, :], worst[:, 0:1], ident[:, :]).then_inc(worst_turned, 1)

                sweeps(pe, sweep)

            @block.scalar
            def _(act):
                act.wait_ge(fold, FOLD_STEPS)

                def copy_norms(k, n, slot):
                    q = q_of(k, n)
                    act.wait_ge(norm_turned, q + 1)
                    if not (k is None and n < 2):
                        act.wait_ge(ln_block, q - 1)
                    nc.scalar.activation(NORM[slot % 2][:, :], psI[1][:, 0, 0:2 * TILES], ACT.Identity).then_inc(norm_copied, 1)

                def copy_in(k, n, slot, g):
                    at = GROUPS * q_of(k, n) + g
                    act.wait_ge(ln_turned, at + 1)
                    nc.scalar.activation(LNT[slot % 2][:, 4 * g:4 * g + 4].rearrange("p j t b -> p j (t b)"), psI[g % 2][:, :, :],
                                         ACT.Identity).then_inc(lnt_copied, 1)

                def sweep(k):
                    slot0 = 0 if k is None else WARM_BLOCKS % 4
                    for n in range(2):
                        copy_norms(k, n, slot0 + n)
                    for g in range(GROUPS):
                        copy_in(k, 0, slot0, g)

                    def steps(n, slot):
                        is_last = fixed(n) and n == n_blocks(k) - 1
                        is_first = fixed(n) and n == 0
                        gi = 0
                        if k is not None and not (fixed(n) and n < 2):
                            act.wait_ge(y_turned, GROUPS * (k * BLOCKS + n - 1))
                        elif k is not None and is_first:
                            act.wait_ge(start_set, k + 2)
                        for t in range(SB):
                            for g in range(2):
                                act.wait_ge(z_ready[g], zcount(k, n, t) + 1)
                                nc.scalar.activation(Y[slot % 2][:, chunks(g), t, :], psZ[g][t % 2][:, 0:HALF].rearrange("p (j b) -> p j b", b=NB),
                                                     ACT.Sigmoid, bias=vec[:, 9:10]).then_inc(y_ready[g], 1)
                                if t == NORM_AT and g == 0 and not (fixed(n) and n + 2 >= n_blocks(k)):
                                    copy_norms(k, n + 2, slot + 2)
                                if g == 0 and not is_last:
                                    for _ in range(IN_AT[t]):
                                        copy_in(k, n + 1, slot + 1, gi)
                                        gi += 1

                    run_blocks(act, k, steps)

                sweeps(act, sweep)

            @block.vector
            def _(v):
                V = nc.vector
                TT, STT = V.tensor_tensor, V.scalar_tensor_tensor
                done = [0]

                def step(ins):
                    done[0] += 1
                    ins.then_inc(fold, 1)
                    v.wait_ge(fold, done[0])
                    return done[0]

                V.memset(minus_half[:, :], -0.5)
                V.memset(ones[:, :], 1.0)
                for buf in NORMS:
                    V.memset(buf[:, :], 0.0)
                V.memset(START[:, :, :], 0.0).then_inc(start_set, 1)
                step(V.memset(NEXT[:, :, :], 0.0))
                v.wait_ge(loaded2, 64)
                v.wait_ge(fold_pe, 1)
                step(V.tensor_copy(w_t[:, :], psI[0][:, 0, :]))
                v.wait_ge(fold_pe, 2)
                assert step(V.tensor_copy(v_t[:, :], psI[1][:, 1, :])) == FOLD_TURNED
                v.wait_ge(fold_pe, 3)
                assert step(TT(prod[:, :], psO[0][:, 0, 0:C], w_t[:, :], ALU.mult)) == FOLD_PROD
                v.wait_ge(fold_pe, 4)
                step(V.tensor_scalar(vec[:, 3:4], psO[1][:, 0, 0:1], 1.0 / NTOK, None, ALU.mult))
                step(TT(vec[:, 4:5], vec[:, 3:4], vec[:, 3:4], ALU.mult))
                v.wait_ge(fold_pe, 5)
                step(STT(vec[:, 5:6], psI[1][:, 0, 0:1], 1.0 / NTOK, vec[:, 4:5], ALU.mult, ALU.subtract))
                assert step(V.tensor_scalar(vec[:, 5:6], vec[:, 5:6], 0.0, BN_EPS, ALU.max, ALU.add)) == FOLD_VAR
                v.wait_ge(fold_pool, 1)
                step(TT(vec[:, 7:8], vec[:, 6:7], vec[:, 0:1], ALU.mult))
                step(TT(vec[:, 8:9], vec[:, 3:4], vec[:, 7:8], ALU.mult))
                step(TT(vec[:, 9:10], vec[:, 1:2], vec[:, 8:9], ALU.subtract))
                assert step(V.tensor_scalar(prod[:, :], w_sb[:, :], vec[:, 7:8], None, ALU.mult)) == FOLD_SCALED
                v.wait_ge(fold_pe, 6)
                assert step(V.tensor_copy(ws_t[:, :], psI[0][:, 0, :])) == FOLD_STEPS

                def sweep(k):
                    def normalise(n, slot, g):
                        q = q_of(k, n)
                        if g == 0:
                            v.wait_ge(norm_copied, q + 1)
                            if not (k is None and n < 2):
                                v.wait_ge(ln_turned, GROUPS * (q - 1))
                        if g % (GROUPS // 2) == 0:
                            v.wait_ge(x_block[(2 * g) // GROUPS], LOADED * (q + 1))
                        for j in range(4 * g, 4 * g + 4):
                            last = V.tensor_scalar(LN[slot % 2][:, j, :], XT[slot % 4][:, j, :], NORM[slot % 2][:, j:j + 1],
                                                   NORM[slot % 2][:, TILES + j:TILES + j + 1], ALU.mult, ALU.add)
                        if g == GROUPS - 1:
                            last.then_inc(ln_block, 1)

                    def add(n, slot, g):
                        at = GROUPS * (k * BLOCKS + n) + g
                        half = (2 * g) // GROUPS
                        v.wait_ge(y_turned, at + 1)
                        if g == half * (GROUPS // 2) and not (fixed(n) and n == 0):
                            v.wait_ge(out_stored[half], 16 * SB * (k * BLOCKS + n))
                        o = OUT[half][:, (4 * g) % (TILES // 2):(4 * g) % (TILES // 2) + 4, :]
                        TT(o, XT[slot % 4][:, 4 * g:4 * g + 4, :], psO[g % 2][:, :, :], ALU.add).then_inc(added, 1)

                    slot0 = 0 if k is None else WARM_BLOCKS % 4
                    for n in range(2):
                        for g in range(GROUPS):
                            normalise(n, slot0 + n, g)

                    def period(n, slot):
                        ahead = not (fixed(n) and n + 2 >= n_blocks(k))
                        behind = k is not None and not (fixed(n) and n == 0)
                        if behind:
                            add(n - 1, slot + 3, 0)
                            add(n - 1, slot + 3, 1)
                        for g in range(GROUPS):
                            if ahead:
                                normalise(n + 2, slot + 2, g)
                            if behind and g + 2 < GROUPS:
                                add(n - 1, slot + 3, g + 2)

                    run_blocks(v, k, period)
                    last_slot = (slot0 + n_blocks(k) - 1) % 4
                    if k is not None:
                        for g in range(GROUPS):
                            add(BLOCKS - 1, last_slot, g)
                    for g in range(2):
                        v.wait_ge(y_ready[g], zcount(k, n_blocks(k), 0))
                    end = Y[last_slot % 2][:, 0:CHUNKS - 1, SB - 1, :]
                    if k is None:
                        V.tensor_copy(START[:, 1:CHUNKS, :], end).then_inc(start_set, 1)
                        V.memset(flag[:, 0:1], 1).then_inc(flag_set, 1)
                        return
                    TT(NEXT[:, 1:CHUNKS, :], end, START[:, 1:CHUNKS, :], ALU.subtract).then_inc(check_step, 1)
                    v.wait_ge(check_step, 2 * k + 1)
                    V.tensor_reduce(worst[:, 0:1], NEXT[:, 1:CHUNKS, :], AX.XY, ALU.max, apply_absolute_value=True).then_inc(check_step, 1)
                    V.tensor_copy(START[:, 1:CHUNKS, :], end).then_inc(start_set, 1)
                    v.wait_ge(worst_turned, k + 1)
                    V.tensor_reduce(worst[0:1, 1:2], psI[0][0:1, 0, :], AX.X, ALU.max).then_inc(worst_max, 1)
                    v.wait_ge(worst_max, k + 1)
                    V.tensor_scalar(flag[0:1, 0:1], worst[0:1, 1:2], START_TOL, None, ALU.is_gt).then_inc(flag_set, 1)

                sweeps(v, sweep)


_OUTS = [((16, 128, 128, 128), "float32")]


def _layouts(inputs):
    import numpy as np

    x = np.ascontiguousarray(inputs["x"])
    rows, width = x.shape[1], x.shape[2]
    a_re, a_im, b_re, b_im = [np.asarray(inputs[f"L0_conv_{n}"]) for n in ("A_real", "A_imag", "B_real", "B_imag")]
    c, k, _ = a_re.shape
    n = k * k
    t = [a.reshape(c, n).T for a in (a_re, a_im, b_re, b_im)]
    taps = np.zeros((128, 5 * c), np.float32)
    taps[0:n] = np.concatenate([t[0], t[1], t[2], t[3], t[3]], 1)
    taps[64:64 + n] = np.concatenate([t[1], t[0], t[3], t[2], t[2]], 1)
    size = width
    pad = (size - k) // 2
    u = np.arange(rows)[:, None, None]
    i, j = np.divmod(np.arange(n), k)
    v = np.arange(width)[None, None, :]
    turns = (u * (i[None, :, None] + pad) + v * (j[None, :, None] + pad)) % size
    dft = np.zeros((rows, 128, width), np.float32)
    dft[:, 0:n] = np.cos(2 * np.pi * turns / size)
    dft[:, 64:64 + n] = np.sin(2 * np.pi * turns / size)
    return {
        "x": x,
        "gate_w": np.concatenate([np.asarray(inputs[f"L0_conv_W{g}"]) for g in "fid"], 1),
        "gate_b": np.concatenate([np.asarray(inputs[f"L0_conv_b{g}"]) for g in "fid"]),
        "taps": taps,
        "dft": dft,
        "row_pick": np.eye(128, 3, dtype=np.float32),
        "ident": np.eye(128, dtype=np.float32),
        "ffn_w": np.ascontiguousarray(inputs["L0_ffn_W"]),
        "ffn_v": np.ascontiguousarray(inputs["L0_ffn_V"]),
        "gamma": np.asarray(inputs["L0_ffn_gamma"]).reshape(128, 1),
        "beta": np.asarray(inputs["L0_ffn_beta"]).reshape(128, 1),
    }


def kernel(**inputs):
    import numpy as _np
    import concourse.bacc as _bacc
    from concourse import mybir as _mybir
    from concourse.bass_utils import run_bass_kernel_spmd as _run

    nc = _bacc.Bacc("TRN2", target_bir_lowering=False, num_devices=1)
    arrays, args = {}, []
    for name, a in _layouts(inputs).items():
        a = _np.ascontiguousarray(a)
        arrays[f"in_{name}_dram"] = a
        args.append(nc.dram_tensor(f"in_{name}_dram", a.shape, _mybir.dt.from_np(a.dtype), kind="ExternalInput").ap())
    for i, (shape, dtype) in enumerate(_OUTS):
        dt = _mybir.dt.from_np(_np.dtype(dtype))
        args.append(nc.dram_tensor(f"out_{i}_dram", shape, dt, kind="ExternalOutput").ap())
    metaformer(nc, *args)
    r = _run(nc, [arrays], core_ids=[0])
    got = tuple(r.results[0][f"out_{i}_dram"] for i in range(len(_OUTS)))
    return got[0]
```
